# Optimizing a Trainium2 kernel written in Bass

```python
import numpy as np
import jax
import jax.numpy as jnp

def _softmax(x, axis=-1):
    return jax.nn.softmax(x, axis=axis)

def _gelu(x):
    return jax.nn.gelu(x, approximate=True)

def _silu(x):
    return jax.nn.silu(x)

def _sigmoid(x):
    return jax.nn.sigmoid(x)

def _layernorm(x, axis=-1, eps=1e-05):
    m = jnp.mean(x, axis=axis, keepdims=True)
    v = jnp.var(x, axis=axis, keepdims=True)
    return (x - m) / jnp.sqrt(v + eps)

def _scatter_add(tgt, idx, src, axis=0):
    return tgt.at[idx].add(src)

def _segment_sum(src, seg, n):
    return jax.ops.segment_sum(src, seg, n)
kernel_name = 'mk_hybrid_d1_jaxref_r8_55ced4'

def setup_inputs(seed: int=0):
    np.random.seed(seed)
    _w = jnp.asarray

    def _L0_attn_a_setup():
        import jax, jax.numpy as jnp
        import numpy as np
        import math
        D_MODEL = 256
        D_STATE = 32
        R_MIN = 0.0
        R_MAX = 0.9
        MAX_PHASE = 6.283185307179586
        B_SZ = 4
        T_LEN = 256
        key = jax.random.key(seed)
        k_x, k_bre, k_bim, k_cre, k_cim = jax.random.split(key, 5)
        x = jax.random.normal(k_x, (B_SZ, T_LEN, D_MODEL), dtype=jnp.float32)
        u = np.linspace(0.0, 1.0, D_STATE, dtype=np.float64)
        mag_init = np.clip(R_MIN + (R_MAX - R_MIN) * u, 1e-06, 1.0 - 1e-06)
        nu_init = -np.log(mag_init)
        nu_log = jnp.asarray(np.log(np.clip(np.expm1(nu_init), 1e-06, None)), dtype=jnp.float32)
        theta_log = jnp.asarray(np.linspace(math.log(0.0001), math.log(MAX_PHASE), D_STATE), dtype=jnp.float32)
        B_re = jax.random.normal(k_bre, (D_STATE, D_MODEL), dtype=jnp.float32) / math.sqrt(D_MODEL)
        B_im = jax.random.normal(k_bim, (D_STATE, D_MODEL), dtype=jnp.float32) / math.sqrt(D_MODEL)
        C_re = jax.random.normal(k_cre, (D_MODEL, D_STATE), dtype=jnp.float32) / math.sqrt(D_STATE)
        C_im = jax.random.normal(k_cim, (D_MODEL, D_STATE), dtype=jnp.float32) / math.sqrt(D_STATE)
        D = jnp.ones((D_MODEL,), dtype=jnp.float32)
        return {'x': x, 'nu_log': nu_log, 'theta_log': theta_log, 'B_re': B_re, 'B_im': B_im, 'C_re': C_re, 'C_im': C_im, 'D': D}
    _L0_attn_a_in = _L0_attn_a_setup()

    def _L0_attn_b_setup():
        import jax, jax.numpy as jnp
        import numpy as np
        EMBED_DIM = 256
        NUM_HEADS = 16
        HEAD_DIM = EMBED_DIM // NUM_HEADS
        B, T = (4, 256)
        key = jax.random.key(seed)
        ks = jax.random.split(key, 9)
        s = 1.0 / np.sqrt(EMBED_DIM)
        x = jax.random.normal(ks[0], (B, T, EMBED_DIM), dtype=jnp.float32)
        Wq = jax.random.normal(ks[1], (EMBED_DIM, EMBED_DIM), dtype=jnp.float32) * s
        bq = jnp.zeros((EMBED_DIM,), dtype=jnp.float32)
        Wk = jax.random.normal(ks[2], (EMBED_DIM, EMBED_DIM), dtype=jnp.float32) * s
        bk = jnp.zeros((EMBED_DIM,), dtype=jnp.float32)
        Wv = jax.random.normal(ks[3], (EMBED_DIM, EMBED_DIM), dtype=jnp.float32) * s
        bv = jnp.zeros((EMBED_DIM,), dtype=jnp.float32)
        Wo = jax.random.normal(ks[4], (EMBED_DIM, EMBED_DIM), dtype=jnp.float32) * s
        bo = jnp.zeros((EMBED_DIM,), dtype=jnp.float32)
        return {'x': x, 'Wq': Wq, 'bq': bq, 'Wk': Wk, 'bk': bk, 'Wv': Wv, 'bv': bv, 'Wo': Wo, 'bo': bo}
    _L0_attn_b_in = _L0_attn_b_setup()

    def _L0_ffn_setup():
        import jax, jax.numpy as jnp
        import numpy as np
        D_MODEL = 256
        D_EXPERT = 1024
        EPS = 1e-08

        def ternary_quant(w):
            scale = jnp.mean(jnp.abs(w)) + EPS
            q = jnp.clip(jnp.round(w / scale), -1.0, 1.0) * scale
            return w + jax.lax.stop_gradient(q - w)
        key = jax.random.key(seed)
        k_x, k_up, k_gate, k_down = jax.random.split(key, 4)
        std_in = 1.0 / np.sqrt(D_MODEL)
        std_exp = 1.0 / np.sqrt(D_EXPERT)
        return {'x': jax.random.normal(k_x, (4, 256, D_MODEL), dtype=jnp.float32), 'W_up': jax.random.normal(k_up, (D_EXPERT, D_MODEL), dtype=jnp.float32) * std_in, 'W_gate': jax.random.normal(k_gate, (D_EXPERT, D_MODEL), dtype=jnp.float32) * std_in, 'W_down': jax.random.normal(k_down, (D_MODEL, D_EXPERT), dtype=jnp.float32) * std_exp}
    _L0_ffn_in = _L0_ffn_setup()
    _d = {'L0_attn_a_x': _L0_attn_a_in['x'], 'L0_attn_a_nu_log': _L0_attn_a_in['nu_log'], 'L0_attn_a_theta_log': _L0_attn_a_in['theta_log'], 'L0_attn_a_B_re': _L0_attn_a_in['B_re'], 'L0_attn_a_B_im': _L0_attn_a_in['B_im'], 'L0_attn_a_C_re': _L0_attn_a_in['C_re'], 'L0_attn_a_C_im': _L0_attn_a_in['C_im'], 'L0_attn_a_D': _L0_attn_a_in['D'], 'L0_attn_b_Wq': _L0_attn_b_in['Wq'], 'L0_attn_b_bq': _L0_attn_b_in['bq'], 'L0_attn_b_Wk': _L0_attn_b_in['Wk'], 'L0_attn_b_bk': _L0_attn_b_in['bk'], 'L0_attn_b_Wv': _L0_attn_b_in['Wv'], 'L0_attn_b_bv': _L0_attn_b_in['bv'], 'L0_attn_b_Wo': _L0_attn_b_in['Wo'], 'L0_attn_b_bo': _L0_attn_b_in['bo'], 'L0_ffn_W_up': _L0_ffn_in['W_up'], 'L0_ffn_W_gate': _L0_ffn_in['W_gate'], 'L0_ffn_W_down': _L0_ffn_in['W_down']}
    _x0 = _d['L0_attn_a_x']
    _d['L0_attn_a_x'] = jax.random.normal(jax.random.fold_in(jax.random.key(seed), 1), (8, 256, 256), dtype=_x0.dtype)
    del _x0
    return _d

def reference(L0_attn_a_x, L0_attn_a_nu_log, L0_attn_a_theta_log, L0_attn_a_B_re, L0_attn_a_B_im, L0_attn_a_C_re, L0_attn_a_C_im, L0_attn_a_D, L0_attn_b_Wq, L0_attn_b_bq, L0_attn_b_Wk, L0_attn_b_bk, L0_attn_b_Wv, L0_attn_b_bv, L0_attn_b_Wo, L0_attn_b_bo, L0_ffn_W_up, L0_ffn_W_gate, L0_ffn_W_down):

    def _L0_attn_a_ref(x, nu_log, theta_log, B_re, B_im, C_re, C_im, D):
        import jax, jax.numpy as jnp
        import numpy as np
        import math
        D_MODEL = 256
        D_STATE = 32
        R_MIN = 0.0
        R_MAX = 0.9
        MAX_PHASE = 6.283185307179586
        B_SZ = 4
        T_LEN = 256
        nu = jax.nn.softplus(nu_log)
        mag = jnp.exp(-jnp.exp(nu))
        theta = jnp.exp(theta_log)
        A_re = mag * jnp.cos(theta)
        A_im = mag * jnp.sin(theta)
        gamma = jnp.sqrt(jnp.clip(1.0 - mag * mag, 0.0))
        gB_re = gamma[:, None] * B_re
        gB_im = gamma[:, None] * B_im
        Bu_re = jnp.einsum('btd,nd->btn', x, gB_re)
        Bu_im = jnp.einsum('btd,nd->btn', x, gB_im)

        def step(h, bu):
            h_re, h_im = h
            bu_re, bu_im = bu
            new_re = A_re * h_re - A_im * h_im + bu_re
            new_im = A_re * h_im + A_im * h_re + bu_im
            return ((new_re, new_im), (new_re, new_im))
        Bsz = x.shape[0]
        h0 = jnp.zeros((Bsz, A_re.shape[0]), dtype=x.dtype)
        _, (H_re, H_im) = jax.lax.scan(step, (h0, h0), (jnp.swapaxes(Bu_re, 0, 1), jnp.swapaxes(Bu_im, 0, 1)))
        H_re = jnp.swapaxes(H_re, 0, 1)
        H_im = jnp.swapaxes(H_im, 0, 1)
        y = jnp.einsum('btn,dn->btd', H_re, C_re) - jnp.einsum('btn,dn->btd', H_im, C_im) + D * x
        return y

    def _L0_attn_b_ref(x, Wq, bq, Wk, bk, Wv, bv, Wo, bo):
        import jax, jax.numpy as jnp
        import numpy as np
        EMBED_DIM = 256
        NUM_HEADS = 16
        HEAD_DIM = EMBED_DIM // NUM_HEADS
        B, T = (4, 256)
        Bb, Tt, C = x.shape
        H, D = (NUM_HEADS, C // NUM_HEADS)
        q = (jnp.einsum('btc,oc->bto', x, Wq) + bq).reshape(Bb, Tt, H, D).transpose(0, 2, 1, 3)
        k = (jnp.einsum('btc,oc->bto', x, Wk) + bk).reshape(Bb, Tt, H, D).transpose(0, 2, 1, 3)
        v = (jnp.einsum('btc,oc->bto', x, Wv) + bv).reshape(Bb, Tt, H, D).transpose(0, 2, 1, 3)
        logits = jnp.einsum('bhqd,bhkd->bhqk', q, k) / jnp.sqrt(jnp.float32(D))
        causal = jnp.triu(jnp.ones((Tt, Tt), dtype=bool), 1)
        logits = jnp.where(causal, -jnp.inf, logits)
        attn = jax.nn.softmax(logits, axis=-1)
        out = jnp.einsum('bhqk,bhkd->bhqd', attn, v)
        out = out.transpose(0, 2, 1, 3).reshape(Bb, Tt, C)
        y = jnp.einsum('btc,oc->bto', out, Wo) + bo
        return y

    def _L0_ffn_ref(x, W_up, W_gate, W_down):
        import jax, jax.numpy as jnp
        import numpy as np
        D_MODEL = 256
        D_EXPERT = 1024
        EPS = 1e-08

        def ternary_quant(w):
            scale = jnp.mean(jnp.abs(w)) + EPS
            q = jnp.clip(jnp.round(w / scale), -1.0, 1.0) * scale
            return w + jax.lax.stop_gradient(q - w)
        wu = ternary_quant(W_up)
        wg = ternary_quant(W_gate)
        wd = ternary_quant(W_down)
        up = jnp.einsum('bsd,ed->bse', x, wu)
        gate = jnp.einsum('bsd,ed->bse', x, wg)
        hidden = jax.nn.silu(up) * gate
        return jnp.einsum('bse,de->bsd', hidden, wd)
    x = L0_attn_a_x
    x = x + _L0_attn_a_ref(_layernorm(x, axis=-1), L0_attn_a_nu_log, L0_attn_a_theta_log, L0_attn_a_B_re, L0_attn_a_B_im, L0_attn_a_C_re, L0_attn_a_C_im, L0_attn_a_D)
    x = x + _L0_ffn_ref(_layernorm(x, axis=-1), L0_ffn_W_up, L0_ffn_W_gate, L0_ffn_W_down)
    x = x + _L0_attn_b_ref(_layernorm(x, axis=-1), L0_attn_b_Wq, L0_attn_b_bq, L0_attn_b_Wk, L0_attn_b_bk, L0_attn_b_Wv, L0_attn_b_bv, L0_attn_b_Wo, L0_attn_b_bo)
    x = x + _L0_ffn_ref(_layernorm(x, axis=-1), L0_ffn_W_up, L0_ffn_W_gate, L0_ffn_W_down)
    return x

_drawn_inputs = setup_inputs


def setup_inputs(seed=0):
    import zlib

    import numpy as np

    out = dict(_drawn_inputs(seed))
    spreads = {'L0_attn_a_D': (1.0, 0.2),
     'L0_attn_b_bq': (0.0, 0.8),
     'L0_attn_b_bk': (0.0, 0.8),
     'L0_attn_b_bv': (0.0, 0.1),
     'L0_attn_b_bo': (0.0, 0.1)}
    factors = {}
    for name, (base, spread) in spreads.items():
        noise = np.random.default_rng([zlib.crc32(name.encode()), seed]).standard_normal(out[name].shape)
        drawn = base * np.exp(spread * noise) if base else spread * noise
        out[name] = jnp.asarray(drawn.astype(out[name].dtype))
    for name, factor in factors.items():
        out[name] = (out[name] * factor).astype(out[name].dtype)
    return out
```

```python
import concourse.bass as bass
from concourse import mybir
from contextlib import ExitStack


def hybrid_block_kernel(nc, x, nu, theta, b_re, b_im, c_re, c_im, dvec,
                        wq, bq, wk, bk, wv, bv, wo, bo, w_up, w_gate, w_down, out):
    F32, F16, BF16, I32 = mybir.dt.float32, mybir.dt.float16, mybir.dt.bfloat16, mybir.dt.int32
    ALU, ACT, AX = mybir.AluOpType, mybir.ActivationFunctionType, mybir.AxisListType

    P = 128
    B, T, D = x.shape
    NS = 2
    TRIPS = B // NS
    TT = T // P
    KD = D // P
    FE = w_up.shape[1]
    NE = FE // P
    H = 16
    HD = D // H
    HT = P // HD
    NST = b_re.shape[1]
    HG = 4
    NG = H // HG
    SLOT = HG * T + HG * P
    CR = 6 * HD
    LN_EPS, Q_EPS = 1e-5, 1e-8
    UP = 2.0 ** 11
    KHID = 0.25 / (UP * UP)
    NEG = -1.0e30
    ROUND = 12582912.0
    ROUND16 = 192.0
    TWO_PI = 6.283185
    Q_PART = (0, 1, 2, 0, 1, 0)
    K_PART = (0, 0, 0, 1, 1, 2)
    NORMS = 4

    DVE_LINKS, POOL_LINKS = 44, 12

    ctx = ExitStack()
    with ctx:
        def sb(name, shape, dt):
            return ctx.enter_context(nc.sbuf_tensor(name, shape, dt))

        def sem(name):
            return ctx.enter_context(nc.semaphore(name))

        wu_q = sb("wu_q", [P, KD, FE], F16)
        wg_q = sb("wg_q", [P, KD, FE], F16)
        wd_q = sb("wd_q", [P, NE, D], F16)
        wq_s = sb("wq_s", [P, KD, D], F32)
        wk_s = sb("wk_s", [P, KD, D], F32)
        wv_s = sb("wv_s", [P, KD, D], F32)
        wo_s = sb("wo_s", [P, NG, D], F32)
        bq_c = sb("bq_c", [P, KD], F32)
        bq4 = sb("bq4", [P, KD], F32)
        bk_c = sb("bk_c", [P, KD], F32)
        bv_b = sb("bv_b", [P, D], F32)
        bo_b = sb("bo_b", [P, D], F32)
        d_b = sb("d_b", [P, D], F32)
        bu_w = sb("bu_w", [P, KD, 2, 2 * NST], F32)
        c_w = sb("c_w", [P, 2, NS, D], F32)
        nu_c = sb("nu_c", [P, 1], F32)
        th_c = sb("th_c", [P, 1], F32)
        sgn = sb("sgn", [P, 1], F32)
        col = sb("col", [P, 16], F32)
        steps_i = sb("steps_i", [P, T], I32)
        steps = sb("steps", [P, T], F32)
        rot_in = sb("rot_in", [P, 2, T], F32)
        rot_out = sb("rot_out", [P, 2, T], F32)
        decay = sb("decay", [P, T], F32)
        ident = sb("ident", [P, P], F32)
        ident_b = sb("ident_b", [P, P], BF16)
        causal = sb("causal", [P, P], BF16)
        ones = sb("ones", [P, P], F32)
        expo = sb("expo", [P, 2], F32)
        wsum = sb("wsum", [P, 4], F32)
        wscale = sb("wscale", [P, 4], F32)
        whalf = sb("whalf", [P, 2, 4], F32)
        k_tanh = sb("k_tanh", [P, 1], F32)
        k_down = sb("k_down", [P, 2], F32)

        xin = sb("xin", [P, NS, TT, D], F32)
        xa = sb("xa", [P, NS, TT, D], F32)
        xb = sb("xb", [P, NS, TT, D], F32)
        xd = sb("xd", [P, NS, TT, D], F32)
        xo = sb("xo", [P, NS, TT, D], F32)
        h = sb("h", [P, NS, TT, D], F32)
        stats = sb("stats", [P, NS, TT, 6], F32)
        mv = sb("mv", [P, NS, TT, 2], F32)
        vs = sb("vs", [P, NS, TT], F32)
        rstd = sb("rstd", [P, NS, TT], F32)
        hT = sb("hT", [P, NS, KD, T], F32)
        hT_hi = sb("hT_hi", [P, NS, KD, T], F16)
        hT_lo = sb("hT_lo", [P, NS, KD, T], F16)
        rec = sb("rec", [P, 4, T], F32)
        rec_o = sb("rec_o", [P, 2, T], F32)
        th = sb("th", [P, 2, 2, T], F32)
        up1 = sb("up1", [P, 2, 2, T], F32)
        hid = sb("hid", [P, 2, 2, T], F32)
        hid_hi = sb("hid_hi", [P, NS, NE, T], F16)
        hid_lo = sb("hid_lo", [P, NS, NE, T], F16)
        qk = sb("qk", [P, NS, 2 * KD, T], F32)
        parts = sb("parts", [P, NS, 3, 2 * KD, T], BF16)
        q_st = sb("q_st", [P, NS, H, T], BF16)
        k_st = sb("k_st", [P, NS, H, T], BF16)
        v_s = sb("v_s", [P, NS, TT, H, 2 * HD], F32)
        nmax = sb("nmax", [P, NS, TT, H], F32)
        nmax_r = sb("nmax_r", [P, 2, TT, H], F32)
        nmax_p = sb("nmax_p", [P, NS, TT, 3, H], BF16)
        nmax_t = sb("nmax_t", [3 * H, NS, T], BF16)

        WN = KD * FE
        stage = sb("stage", [P, 3 * WN], F32)
        wu_f = stage[:, 0:WN].rearrange("p (k e) -> p k e", k=KD)
        wg_f = stage[:, WN:2 * WN].rearrange("p (k e) -> p k e", k=KD)
        wd_f = stage[:, 2 * WN:3 * WN].rearrange("p (k e) -> p k e", k=NE)
        pexp = stage[:, 0:2 * SLOT].rearrange("p (b n) -> p b n", b=2)
        psum_b = stage[:, 2 * SLOT:2 * SLOT + 4 * T].rearrange("p (b n) -> p b n", b=2)
        qk_r = stage[:, 2 * WN:2 * WN + NS * 2 * KD * T].rearrange("p (s k t) -> p s k t", s=NS, k=2 * KD)
        late = sb("late", [P, 2 * WN], F32)
        oT = late[:, 0:NS * NG * T].rearrange("p (s g t) -> p s g t", s=NS, g=NG)
        absw = late[:, 0:WN]
        below = late[:, WN:WN + WN // 2].bitcast(F16)
        turn = late[:, WN + WN // 2:WN + WN // 2 + 3 * T].rearrange("p (a t) -> p a t", a=3)
        sin_t, cos_t = xo[:, 0, 0], xo[:, 0, 1]

        scratch = nc.dram_tensor("qk_parts", (NS, 3, 2 * KD, P, T), BF16, kind="Internal").ap()

        work = [ctx.enter_context(nc.psum_tensor(f"work{i}", [P, 3, 512], F32)) for i in range(2)]
        side = [ctx.enter_context(nc.psum_tensor(f"side{i}", [P, 512], F32)) for i in range(2)]

        s_w = sem("weights_in")
        s_wf = [sem(f"ffn_weight{i}_in") for i in range(3)]
        s_const = sem("constants_ready")
        s_zero = sem("padding_zeroed")
        s_abs = sem("weight_abs_sums")
        s_tot = sem("weight_totals")
        s_quant = sem("weights_quantised")
        s_gam = sem("gamma_ready")
        s_mag = sem("mag_ready")
        s_theta = sem("theta_ready")
        s_phase = sem("phases_ready")
        s_sin = sem("sines_ready")
        s_tab = sem("tables_ready")
        s_omg = sem("gamma_square_ready")
        s_dl, s_al, s_pl = sem("dve_links"), sem("act_links"), sem("pool_links")

        s_x = sem("x_in")
        s_mv = sem("moments_ready")
        s_rstd = sem("rstd_ready")
        s_h = sem("normed_ready")
        s_tr = sem("transposed")
        s_hi = sem("hT_high_ready")
        s_lo = sem("hT_low_ready")
        s_bu = sem("bu_done")
        s_rec = sem("recurrence_done")
        s_y = sem("recurrence_out_done")
        s_xd = sem("skip_ready")
        s_ug = sem("up_gate_done")
        s_th = sem("tanh_done")
        s_hid = sem("hidden_done")
        s_hhi = sem("hidden_high_ready")
        s_hlo = sem("hidden_low_ready")
        s_dn = sem("down_done")
        s_x2 = sem("ffn_residual_ready")
        s_qk = sem("qk_done")
        s_v = sem("v_done")
        s_vr = sem("v_ready")
        s_p0, s_r1, s_p1, s_p2 = sem("part0_ready"), sem("rest1_ready"), sem("part1_ready"), sem("part2_ready")
        s_sw = [sem(f"scratch_written{s}") for s in range(NS)]
        s_st = [sem(f"stack_in{s}") for s in range(NS)]
        s_s = sem("scores_done")
        s_max = sem("max_done")
        s_mp = sem("max_parts_ready")
        s_mt = sem("max_transposed")
        s_ms = sem("max_rows_ready")
        s_mr = [sem(f"max_rows_in{s}") for s in range(NS)]
        s_lt = sem("logits_t_done")
        s_exp = sem("exp_done")
        s_msk = sem("masked")
        s_pv = sem("pv_done")
        s_on = sem("heads_normalised")
        s_xbo = sem("bias_added")
        s_wo = sem("wo_done")
        s_out = sem("out_written")
        s_xo = sem("out_ready")

        N_SMALL = 0
        small = [
            (wq_s[:, :, :], wq.rearrange("(k p) o -> p k o", p=P)),
            (wk_s[:, :, :], wk.rearrange("(k p) o -> p k o", p=P)),
            (wv_s[:, :, :], wv.rearrange("(k p) o -> p k o", p=P)),
            (bq_c[:, :], bq), (bk_c[:, :], bk),
            (bv_b[:, :], bv.partition_broadcast(P)), (bo_b[:, :], bo.partition_broadcast(P)),
            (d_b[:, :], dvec.partition_broadcast(P)),
            (bu_w[:, :, 0, 0:NST], b_re.rearrange("(k p) n -> p k n", p=P)),
            (bu_w[:, :, 0, NST:], b_im.rearrange("(k p) n -> p k n", p=P)),
            (bu_w[:, :, 1, 0:NST], b_im.rearrange("(k p) n -> p k n", p=P)),
            (bu_w[:, :, 1, NST:], b_re.rearrange("(k p) n -> p k n", p=P)),
        ]
        padded = []
        for j in range(HG):
            padded.append((wo_s[32 * j:32 * j + HD, :, :],
                           wo.rearrange("(g j i) d -> j i g d", j=HG, i=HD)[j]))
        for s in range(NS):
            for half in range(2):
                r = 2 * NST * s + NST * half
                padded.append((c_w[r:r + NST, 0, s, :], (c_re, c_im)[half]))
                padded.append((c_w[r:r + NST, 1, s, :], (c_im, c_re)[half]))

        def settled(eng):
            eng.nop(nofuse=True)

        block = ctx.enter_context(nc.Block())

        @block.sync
        def _(sp):
            sp.dma_start(nu_c[:, :], nu).then_inc(s_x, 16)
            sp.dma_start(th_c[:, :], theta).then_inc(s_x, 16)
            sp.wait_ge(s_x, 32)
            x_v = x.rearrange("(i s) (t p) d -> i p (s t) d", s=NS, p=P)
            o_v = out.rearrange("(i s) (t p) d -> i p (s t) d", s=NS, p=P)
            xin_v = xin[:, :, :, :].rearrange("p s t d -> p (s t) d")
            sp.dma_start(xin_v, x_v[0]).then_inc(s_x, 16)
            for dst, src in small:
                sp.dma_start(dst, src).then_inc(s_w, 16)
            sp.wait_ge(s_zero, 2)
            for dst, src in padded:
                sp.dma_start(dst, src).then_inc(s_w, 16)
            for n, (dst, src) in enumerate(((wu_f, w_up), (wg_f, w_gate), (wd_f, w_down))):
                sp.dma_start(dst[:, :, :], src.rearrange("(k p) e -> p k e", p=P)).then_inc(s_wf[n], 16)

            def trip(i, last):
                if not last:
                    sp.wait_ge(s_xd, i + 1)
                    sp.wait_ge(s_h, i * NORMS * NS + 2)
                    sp.dma_start(xin_v, x_v[i + 1]).then_inc(s_x, 16)
                for s in range(NS):
                    sp.wait_ge(s_p2, i * NS + s + 1)
                    sp.dma_start(scratch[s].rearrange("a k p t -> p (a k) t"),
                                 parts[:, s].rearrange("p a k t -> p (a k) t")).then_inc(s_sw[s], 16)
                    sp.wait_ge(s_sw[s], i * 16 + 16)
                    for c in range(6):
                        for stack, part, base in ((q_st, Q_PART[c], 0), (k_st, K_PART[c], KD)):
                            sp.dma_start(stack[c * HD:(c + 1) * HD, s].rearrange("i (k g) t -> i k (g t)", k=KD),
                                         scratch[s, part, base:base + KD].rearrange("k (i g) t -> i k (g t)", g=HT)
                                         ).then_inc(s_st[s], 16)
                for s in range(NS):
                    sp.wait_ge(s_ms, i * NS + s + 1)
                    for a in range(3):
                        sp.dma_start(q_st[CR + a:CR + a + 1, s],
                                     nmax_t[a * H:(a + 1) * H, s]).then_inc(s_mr[s], 16)
                for s in range(NS):
                    sp.wait_ge(s_xo, i * NS + s + 1)
                    sp.dma_start(o_v[i][:, s * TT:(s + 1) * TT, :], xo[:, s]).then_inc(s_out, 16)
                sp.wait_ge(s_out, (i * NS + NS) * 16)
                settled(sp)

            with nc.sync.Fori(0, TRIPS - 1) as i:
                trip(i, False)
            trip(TRIPS - 1, True)

        @block.gpsimd
        def _(pool):
            g = nc.gpsimd
            n = [0]

            def link(ins, base=0):
                n[0] += 1
                ins.then_inc(s_pl, 1)
                pool.wait_ge(s_pl, base + n[0])

            g.memset(wo_s[:, :, :], 0.0).then_inc(s_zero, 1)
            g.memset(c_w[:, :, :, :], 0.0).then_inc(s_zero, 1)
            g.memset(expo[:, 0:1], -0.5)
            g.memset(expo[:, 1:2], 0.5)
            g.memset(ones[:, :], 1.0)
            g.memset(v_s[:, :, :, :, :], 1.0)
            g.iota(steps_i[:, :], pattern=[[1, T]], base=0, channel_multiplier=0)
            g.memset(k_st[:, :, :, :], 1.0)
            g.memset(ident_b[:, :], 0.0)
            g.memset(causal[:, :], 0.0)
            link(g.memset(ident[:, :], 0.0))
            link(g.tensor_copy(steps[:, :], steps_i[:, :]))
            g.affine_select(out=ident_b[:, :], in_=ident_b[:, :], compare_op=ALU.not_equal, fill=1.0, base=0,
                            pattern=[[-1, P]], channel_multiplier=1)
            g.affine_select(out=causal[:, :], in_=causal[:, :], compare_op=ALU.is_ge, fill=NEG, base=0,
                            pattern=[[-1, P]], channel_multiplier=1)
            g.affine_select(out=ident[:, :], in_=ident[:, :], compare_op=ALU.not_equal, fill=1.0, base=0,
                            pattern=[[-1, P]], channel_multiplier=1).then_inc(s_const, 1)
            pool.wait_ge(s_omg, 1)
            g.tensor_tensor(col[:, 5:6], col[:, 4:5], expo[:, 1:2], ALU.pow).then_inc(s_gam, 1)
            start = n[0]

            def norm_rstd(i, k, scale):
                s = k % NS
                base = start + i * POOL_LINKS - start
                pool.wait_ge(s_mv, i * NORMS * NS + k + 1)
                settled(pool)
                link(g.tensor_scalar(vs[:, s], mv[:, s, :, 1], LN_EPS, scale ** -2, ALU.add, ALU.mult), i * POOL_LINKS)
                g.tensor_tensor(rstd[:, s], vs[:, s], expo[:, 0:1].to_broadcast([P, TT]),
                                ALU.pow).then_inc(s_rstd, 1)

            def ffn_low(i, f):
                for u in range(NS * NE // 2):
                    s, e = u // (NE // 2), 2 * (u % (NE // 2))
                    k = f * NS * NE // 2 + u
                    pool.wait_ge(s_hhi, i * NS * NE + k + 1)
                    g.tensor_tensor(hid_lo[:, s, e:e + 2], hid[:, u % 2], hid_hi[:, s, e:e + 2],
                                    ALU.subtract).then_inc(s_hlo, 1)

            with nc.gpsimd.Fori(0, TRIPS) as i:
                n[0] = start
                for s in range(NS):
                    norm_rstd(i, s, 1.0)
                for s in range(NS):
                    pool.wait_ge(s_h, i * NORMS * NS + s + 1)
                    last = None
                    for t in range(TT):
                        link(g.tensor_tensor(xd[:, s, t], h[:, s, t], d_b[:, :], ALU.mult), i * POOL_LINKS)
                        last = g.tensor_tensor(xd[:, s, t], xd[:, s, t], xin[:, s, t], ALU.add)
                last.then_inc(s_xd, 1)
                for s in range(NS):
                    norm_rstd(i, NS + s, UP)
                ffn_low(i, 0)
                for s in range(NS):
                    norm_rstd(i, 2 * NS + s, 1.0)
                    for t in range(TT):
                        ins = g.tensor_tensor(xa[:, s, t], xb[:, s, t], bo_b[:, :], ALU.add)
                    ins.then_inc(s_xbo, 1)
                for k in range(NS * NG):
                    pool.wait_ge(s_exp, i * NS * NG + k + 1)
                    settled(pool)
                    b = k % 2
                    g0 = pexp[:, b, 0:HG * T].rearrange("p (h q) -> p h q", h=HG)[:, :, 0:P]
                    g1 = pexp[:, b, HG * T:SLOT].rearrange("p (h q) -> p h q", h=HG)
                    for v in (g0, g1):
                        ins = g.affine_select(out=v, in_=v, compare_op=ALU.is_ge, fill=0.0, base=0,
                                              pattern=[[0, HG], [1, P]], channel_multiplier=-1)
                    ins.then_inc(s_msk, 1)
                for s in range(NS):
                    norm_rstd(i, 3 * NS + s, UP)
                ffn_low(i, 1)
                assert n[0] - start == POOL_LINKS, n[0] - start

        @block.scalar
        def _(act):
            a = nc.scalar
            act.wait_ge(s_x, 32)
            a.activation(col[:, 0:1], nu_c[:, :], ACT.Exp)
            a.activation(col[:, 1:2], th_c[:, :], ACT.Exp).then_inc(s_theta, 1)
            act.wait_ge(s_mag, 1)
            a.activation(col[:, 3:4], col[:, 2:3], ACT.Exp).then_inc(s_theta, 1)
            act.wait_ge(s_phase, 1)
            a.activation(sin_t[:, :], turn[:, 0], ACT.Sin, scale=TWO_PI)
            a.activation(cos_t[:, :], turn[:, 1], ACT.Sin, scale=TWO_PI).then_inc(s_sin, 1)
            for n, w in enumerate((wu_f, wg_f, wd_f)):
                act.wait_ge(s_wf[n], 16)
                if n:
                    act.wait_ge(s_abs, n)
                a.activation(absw[:, :], w[:, :, :].rearrange("p k e -> p (k e)"), ACT.Abs,
                             accum_out=wsum[:, n:n + 1]).then_inc(s_abs, 1)

            def copy_hT(i, k, dst):
                s = k % NS
                act.wait_ge(s_tr, i * NORMS * NS + k + 1)
                a.copy(dst[:, s], side[s][:, :].rearrange("p (k t) -> p k t", k=KD)).then_inc(s_hi, 1)

            def ffn_act(i, f):
                def high(u):
                    s, e = u // (NE // 2), 2 * (u % (NE // 2))
                    act.wait_ge(s_hid, i * NS * NE + f * NS * NE // 2 + u + 1)
                    a.copy(hid_hi[:, s, e:e + 2], hid[:, u % 2]).then_inc(s_hhi, 1)

                for u in range(NS * NE // 2):
                    k = f * NS * NE // 2 + u
                    if u == NE // 2:
                        copy_hT(i, (2 * f + 1) * NS + 1, hT_hi)
                    act.wait_ge(s_ug, i * NS * NE + k + 1)
                    if u >= 2:
                        act.wait_ge(s_hid, i * NS * NE + k - 1)
                    a.activation(th[:, u % 2], work[u % 2][:, 0:2, 0:T], ACT.Tanh,
                                 scale=k_tanh[:, 0:1]).then_inc(s_th, 1)
                    if u >= 1:
                        high(u - 1)
                high(NS * NE // 2 - 1)

            act.wait_ge(s_tab, 1)
            act.wait_ge(s_w, 16 * (len(small) + len(padded)))
            a.activation(bq4[:, :], bq_c[:, :], ACT.Copy, scale=HD ** -0.5).then_inc(s_al, 1)
            act.wait_ge(s_al, 1)
            with nc.scalar.Fori(0, TRIPS) as i:
                for s in range(NS):
                    copy_hT(i, s, hT)
                copy_hT(i, NS, hT_hi)
                ffn_act(i, 0)
                for s in range(NS):
                    copy_hT(i, 2 * NS + s, hT)
                for s in range(NS):
                    act.wait_ge(s_qk, i * NS + s + 1)
                    for t in range(KD):
                        a.activation(qk[:, s, t], work[s][:, 0, t * T:(t + 1) * T], ACT.Identity,
                                     bias=bq4[:, t:t + 1], scale=HD ** -0.5)
                    for t in range(KD):
                        ins = a.activation(qk[:, s, KD + t], work[s][:, 1, t * T:(t + 1) * T], ACT.Identity,
                                           bias=bk_c[:, t:t + 1])
                    ins.then_inc(s_al, 1)
                    act.wait_ge(s_al, i * NS + s + 2)
                    a.copy(parts[:, s, 0], qk[:, s]).then_inc(s_p0, 1)
                    act.wait_ge(s_r1, i * NS + s + 1)
                    a.copy(parts[:, s, 1], qk_r[:, s]).then_inc(s_p1, 1)
                for s in range(NS):
                    act.wait_ge(s_mt, i * NS + s + 1)
                    a.copy(nmax_t[:, s], side[s][0:3 * H, 0:P].bitcast(BF16)).then_inc(s_ms, 1)
                for k in range(NS * NG):
                    act.wait_ge(s_lt, i * NS * NG + k + 1)
                    if k >= 2:
                        act.wait_ge(s_pv, i * NS * NG + k - 1)
                    a.activation(pexp[:, k % 2], work[k % 2][:, :, :].rearrange("p a b -> p (a b)"),
                                 ACT.Exp).then_inc(s_exp, 1)
                copy_hT(i, 3 * NS, hT_hi)
                ffn_act(i, 1)

        @block.vector
        def _(dve):
            v = nc.vector
            n = [0]
            per = [0]

            def link(ins):
                n[0] += 1
                ins.then_inc(s_dl, 1)
                dve.wait_ge(s_dl, per[0] + n[0])

            for s in range(NS):
                v.memset(sgn[2 * NST * s:2 * NST * s + NST, :], 1.0)
                v.memset(sgn[2 * NST * s + NST:2 * NST * (s + 1), :], -1.0)
            dve.wait_ge(s_theta, 1)
            v.tensor_scalar(col[:, 2:3], col[:, 0:1], -1.0, -1.0, ALU.mult, ALU.add).then_inc(s_mag, 1)
            link(v.tensor_scalar(col[:, 6:7], col[:, 1:2], 0.15915494309189535, None, ALU.mult))
            link(v.tensor_scalar(col[:, 7:8], col[:, 6:7], ROUND, ROUND, ALU.add, ALU.subtract))
            link(v.tensor_tensor(col[:, 8:9], col[:, 6:7], col[:, 7:8], ALU.subtract))
            link(v.tensor_scalar(col[:, 9:10], col[:, 8:9], ROUND16, ROUND16, ALU.add, ALU.subtract))
            link(v.tensor_tensor(col[:, 10:11], col[:, 8:9], col[:, 9:10], ALU.subtract))
            dve.wait_ge(s_const, 1)
            link(v.tensor_scalar(turn[:, 0], steps[:, :], col[:, 9:10], None, ALU.mult))
            link(v.tensor_scalar(turn[:, 1], turn[:, 0], ROUND, ROUND, ALU.add, ALU.subtract))
            link(v.tensor_tensor(turn[:, 2], turn[:, 0], turn[:, 1], ALU.subtract))
            link(v.scalar_tensor_tensor(turn[:, 1], steps[:, :], col[:, 10:11], turn[:, 2], ALU.mult, ALU.add))
            link(v.tensor_scalar(turn[:, 2], turn[:, 1], ROUND, ROUND, ALU.add, ALU.subtract))
            link(v.tensor_tensor(turn[:, 0], turn[:, 1], turn[:, 2], ALU.subtract))
            link(v.tensor_scalar(turn[:, 1], turn[:, 0], 0.25, None, ALU.add))
            link(v.tensor_scalar(turn[:, 2], turn[:, 1], ROUND, ROUND, ALU.add, ALU.subtract))
            v.tensor_tensor(turn[:, 1], turn[:, 1], turn[:, 2], ALU.subtract).then_inc(s_phase, 1)
            dve.wait_ge(s_theta, 2)
            link(v.tensor_scalar(col[:, 11:12], col[:, 3:4], col[:, 3:4], -1.0, ALU.mult, ALU.mult))
            v.tensor_scalar(col[:, 4:5], col[:, 11:12], 1.0, 0.0, ALU.add, ALU.max).then_inc(s_omg, 1)
            v.tensor_scalar(decay[:, :], steps[:, :], 0.0, col[:, 3:4], ALU.mult, ALU.add)
            dve.wait_ge(s_gam, 1)
            link(v.tensor_tensor(col[:, 12:13], col[:, 5:6], sgn[:, :], ALU.mult))
            dve.wait_ge(s_sin, 1)
            v.tensor_scalar(rot_in[:, 0], cos_t[:, :], col[:, 5:6], None, ALU.mult)
            v.tensor_scalar(rot_in[:, 1], sin_t[:, :], col[:, 12:13], None, ALU.mult)
            v.tensor_scalar(rot_out[:, 0], cos_t[:, :], sgn[:, 0:1], None, ALU.mult)
            link(v.tensor_scalar(rot_out[:, 1], sin_t[:, :], -1.0, None, ALU.mult))

            for m, (w, q) in enumerate(((wu_f, wu_q), (wg_f, wg_q), (wd_f, wd_q))):
                dve.wait_ge(s_tot, m + 1)
                link(v.tensor_scalar(wscale[:, m:m + 1], work[0][:, m, 0:1], 1.0 / (D * FE), Q_EPS,
                                     ALU.mult, ALU.add))
                v.tensor_scalar(whalf[:, 0, m:m + 1], wscale[:, m:m + 1], 0.5, None, ALU.mult)
                link(v.tensor_scalar(whalf[:, 1, m:m + 1], wscale[:, m:m + 1], -0.5, None, ALU.mult))
                wf, qf = (z[:, :, :].rearrange("p k e -> p (k e)") for z in (w, q))
                link(v.tensor_scalar(below[:, :], wf, whalf[:, 1, m:m + 1], None, ALU.is_lt))
                v.scalar_tensor_tensor(qf, wf, whalf[:, 0, m:m + 1], below[:, :], ALU.is_gt,
                                       ALU.subtract).then_inc(s_quant, 1)
                dve.wait_ge(s_quant, m + 1)
            v.tensor_scalar(k_tanh[:, :], wscale[:, 0:1], 0.5 / UP, None, ALU.mult)
            link(v.tensor_scalar(k_down[:, 0:1], wscale[:, 0:1], wscale[:, 1:2], 2.0, ALU.mult, ALU.mult))
            link(v.tensor_scalar(k_down[:, 1:2], k_down[:, 0:1], wscale[:, 2:3], None, ALU.mult))
            v.memset(col[:, 15:16], 0.0).then_inc(s_tab, 1)
            dve.wait_ge(s_w, 16 * (len(small) + len(padded)))
            start = n[0]

            def moments(i, k, src):
                s = k % NS
                for t in range(TT):
                    ins = v.bn_stats(stats[:, s, t], src[:, s, t])
                link(ins)
                settled(dve)
                for t in range(TT):
                    ins = v.bn_aggr(mv[:, s, t], stats[:, s, t])
                ins.then_inc(s_mv, 1)

            def normalise(i, k, src):
                s = k % NS
                dve.wait_ge(s_rstd, i * NORMS * NS + k + 1)
                for t in range(TT):
                    ins = v.tensor_scalar(h[:, s, t], src[:, s, t], mv[:, s, t, 0:1], rstd[:, s, t:t + 1],
                                          ALU.subtract, ALU.mult)
                ins.then_inc(s_h, 1)

            def low(i, k):
                s = k % NS
                dve.wait_ge(s_hi, i * NORMS * NS + k + 1)
                v.tensor_tensor(hT_lo[:, s], side[s][:, :].rearrange("p (k t) -> p k t", k=KD), hT_hi[:, s],
                                ALU.subtract).then_inc(s_lo, 1)

            def ffn_dve(i, f, src, dst, done):
                for u in range(NS * NE // 2):
                    k = f * NS * NE // 2 + u
                    if u == NE // 2:
                        low(i, (2 * f + 1) * NS + 1)
                    dve.wait_ge(s_th, i * NS * NE + k + 1)
                    if u >= 2:
                        dve.wait_ge(s_hlo, i * NS * NE + k - 1)
                    link(v.scalar_tensor_tensor(up1[:, u % 2], th[:, u % 2], 1.0, work[u % 2][:, 0:2, 0:T],
                                                ALU.add, ALU.mult))
                    v.scalar_tensor_tensor(hid[:, u % 2], up1[:, u % 2], KHID, work[u % 2][:, 0:2, T:2 * T],
                                           ALU.mult, ALU.mult).then_inc(s_hid, 1)
                for s in range(NS):
                    dve.wait_ge(s_dn, i * 2 * NS + f * NS + s + 1)
                    v.scalar_tensor_tensor(dst[:, s].rearrange("p t d -> p (t d)"), side[s][:, :],
                                           k_down[:, 1:2], src[:, s].rearrange("p t d -> p (t d)"),
                                           ALU.mult, ALU.add).then_inc(done, 1)
                    if f == 0:
                        dve.wait_ge(done, i * NS + s + 1)
                        moments(i, 2 * NS + s, dst)
                if f == 0:
                    for s in range(NS):
                        normalise(i, 2 * NS + s, dst)

            with nc.vector.Fori(0, TRIPS) as i:
                n[0] = start
                per[0] = i * DVE_LINKS
                dve.wait_ge(s_x, i * 16 + 48)
                for s in range(NS):
                    moments(i, s, xin)
                for s in range(NS):
                    normalise(i, s, xin)
                dve.wait_ge(s_bu, i + 1)
                v.tensor_tensor(rec[:, 0], work[0][:, 0, 0:T], rot_in[:, 0], ALU.mult)
                link(v.tensor_tensor(rec[:, 1], work[0][:, 1, 0:T], rot_in[:, 1], ALU.mult))
                link(v.tensor_tensor(rec[:, 2], rec[:, 0], rec[:, 1], ALU.add))
                link(v.tensor_tensor_scan(rec[:, 3], decay[:, :], rec[:, 2], 0.0, ALU.mult, ALU.add))
                v.tensor_tensor(rec_o[:, 0], rec[:, 3], rot_out[:, 0], ALU.mult)
                v.tensor_tensor(rec_o[:, 1], rec[:, 3], rot_out[:, 1], ALU.mult).then_inc(s_rec, 1)
                dve.wait_ge(s_xd, i + 1)
                for t in range(TT):
                    dve.wait_ge(s_y, i * TT + t + 1)
                    ins = v.tensor_tensor(xa[:, :, t], side[t][:, :].rearrange("p (s d) -> p s d", s=NS),
                                          xd[:, :, t], ALU.add)
                link(ins)
                for s in range(NS):
                    moments(i, NS + s, xa)
                for s in range(NS):
                    normalise(i, NS + s, xa)
                low(i, NS)
                ffn_dve(i, 0, xa, xb, s_x2)
                for s in range(NS):
                    dve.wait_ge(s_v, i * NS + s + 1)
                    for t in range(TT):
                        ins = v.tensor_tensor(v_s[:, s, t, :, 0:HD],
                                              work[s][:, 2, t * D:(t + 1) * D].rearrange("p (h d) -> p h d", h=H),
                                              bv_b[:, :].rearrange("p (h d) -> p h d", h=H), ALU.add)
                    ins.then_inc(s_vr, 1)
                    dve.wait_ge(s_p0, i * NS + s + 1)
                    v.tensor_tensor(qk_r[:, s], qk[:, s], parts[:, s, 0], ALU.subtract).then_inc(s_r1, 1)
                    dve.wait_ge(s_p1, i * NS + s + 1)
                    v.tensor_tensor(parts[:, s, 2], qk_r[:, s], parts[:, s, 1], ALU.subtract).then_inc(s_p2, 1)
                for s in range(NS):
                    for g in range(NG):
                        k = s * NG + g
                        dve.wait_ge(s_s, i * NS * NG + k + 1)
                        w = work[g % 2]
                        v.tensor_reduce(nmax[:, s, 1, g * HG:(g + 1) * HG],
                                        w[:, 0:2, :].rearrange("p a (h k) -> p (a h) k", k=T), AX.X, ALU.max,
                                        negate=True)
                        v.tensor_reduce(nmax[:, s, 0, g * HG:(g + 1) * HG],
                                        w[:, 2, :].rearrange("p (h k) -> p h k", k=P), AX.X, ALU.max,
                                        negate=True).then_inc(s_max, 1)
                    dve.wait_ge(s_max, i * NS * NG + (s + 1) * NG)
                    link(v.tensor_copy(nmax_p[:, s, :, 0], nmax[:, s]))
                    link(v.tensor_tensor(nmax_r[:, 0], nmax[:, s], nmax_p[:, s, :, 0], ALU.subtract))
                    link(v.tensor_copy(nmax_p[:, s, :, 1], nmax_r[:, 0]))
                    v.tensor_tensor(nmax_p[:, s, :, 2], nmax_r[:, 0], nmax_p[:, s, :, 1],
                                    ALU.subtract).then_inc(s_mp, 1)
                for k in range(NS * 2):
                    s, half = k // 2, k % 2
                    dve.wait_ge(s_pv, i * NS * NG + 2 * k + 2)
                    settled(dve)
                    link(v.stream_shuffle(psum_b[:, k % 2], side[half][:, :], [HD] * 32))
                    link(v.reciprocal(psum_b[:, k % 2], psum_b[:, k % 2]))
                    v.tensor_tensor(oT[:, s, 2 * half:2 * half + 2].rearrange("p g t -> p (g t)"),
                                    side[half][:, :], psum_b[:, k % 2], ALU.mult).then_inc(s_on, 1)
                for s in range(NS):
                    dve.wait_ge(s_wo, i * NS + s + 1)
                    dve.wait_ge(s_xbo, i * NS + s + 1)
                    link(v.tensor_tensor(xb[:, s].rearrange("p t d -> p (t d)"), side[s][:, :],
                                         xa[:, s].rearrange("p t d -> p (t d)"), ALU.add))
                    moments(i, 3 * NS + s, xb)
                for s in range(NS):
                    normalise(i, 3 * NS + s, xb)
                low(i, 3 * NS)
                ffn_dve(i, 1, xb, xo, s_xo)
                assert n[0] - start == DVE_LINKS, n[0] - start

        @block.tensor
        def _(pe):
            t_ = nc.tensor
            pe.wait_ge(s_const, 1)
            for n in range(3):
                pe.wait_ge(s_abs, n + 1)
                t_.matmul(work[0][:, n, 0:1], ones[:, :], wsum[:, n:n + 1], start=True, stop=True).then_inc(s_tot, 1)
            pe.wait_ge(s_w, 16 * (len(small) + len(padded)))
            pe.wait_ge(s_quant, 3)

            def transpose_h(i, k):
                s = k % NS
                pe.wait_ge(s_h, i * NORMS * NS + k + 1)
                for t in range(TT):
                    for c in range(KD):
                        ins = t_.transpose(side[s][:, c * T + t * P:c * T + (t + 1) * P],
                                           h[:, s, t, c * P:(c + 1) * P], ident[:, :])
                ins.then_inc(s_tr, 1)

            def up_gate(i, f, s):
                pe.wait_ge(s_hi, i * NORMS * NS + (2 * f + 1) * NS + s + 1)
                pe.wait_ge(s_lo, i * 2 * NS + f * NS + s + 1)
                for u in range(NE // 2):
                    k = f * NS * NE // 2 + s * NE // 2 + u
                    if s * NE // 2 + u >= 2:
                        pe.wait_ge(s_hid, i * NS * NE + k - 1)
                    for j in range(2):
                        e = 2 * u + j
                        for c0, w in ((0, wu_q), (T, wg_q)):
                            for c in range(KD):
                                for part, src in ((0, hT_hi), (1, hT_lo)):
                                    ins = t_.matmul(work[u % 2][:, j, c0:c0 + T], w[:, c, e * P:(e + 1) * P],
                                                    src[:, s, c], start=(c == 0 and part == 0),
                                                    stop=(c == KD - 1 and part == 1))
                    ins.then_inc(s_ug, 1)

            def down(i, f, s):
                pe.wait_ge(s_hhi, i * NS * NE + f * NS * NE // 2 + (s + 1) * NE // 2)
                pe.wait_ge(s_hlo, i * NS * NE + f * NS * NE // 2 + (s + 1) * NE // 2)
                for t in range(TT):
                    for e in range(NE):
                        for part, src in ((0, hid_hi), (1, hid_lo)):
                            ins = t_.matmul(side[s][:, t * D:(t + 1) * D], src[:, s, e, t * P:(t + 1) * P],
                                            wd_q[:, e], start=(e == 0 and part == 0),
                                            stop=(e == NE - 1 and part == 1))
                ins.then_inc(s_dn, 1)

            def ffn(i, f):
                transpose_h(i, (2 * f + 1) * NS)
                up_gate(i, f, 0)
                transpose_h(i, (2 * f + 1) * NS + 1)
                up_gate(i, f, 1)
                for s in range(NS):
                    down(i, f, s)

            with nc.tensor.Fori(0, TRIPS) as i:
                for s in range(NS):
                    transpose_h(i, s)
                for s in range(NS):
                    pe.wait_ge(s_hi, i * NORMS * NS + s + 1)
                    r = 2 * NST * s
                    for m in range(2):
                        for c in range(KD):
                            ins = t_.matmul(work[0][r:r + 2 * NST, m, 0:T], bu_w[:, c, m], hT[:, s, c],
                                            start=(c == 0), stop=(c == KD - 1))
                ins.then_inc(s_bu, 1)
                pe.wait_ge(s_rec, i + 1)
                for t in range(TT):
                    for m in range(2):
                        ins = t_.matmul(side[t][:, :], rec_o[:, m, t * P:(t + 1) * P],
                                        c_w[:, m].rearrange("p s d -> p (s d)"), start=(m == 0), stop=(m == 1))
                    ins.then_inc(s_y, 1)
                ffn(i, 0)
                for s in range(NS):
                    transpose_h(i, 2 * NS + s)
                for s in range(NS):
                    pe.wait_ge(s_hi, i * NORMS * NS + 2 * NS + s + 1)
                    for m, w in ((0, wq_s), (1, wk_s)):
                        for t in range(KD):
                            for c in range(KD):
                                ins = t_.matmul(work[s][:, m, t * T:(t + 1) * T], w[:, c, t * P:(t + 1) * P],
                                                hT[:, s, c], start=(c == 0), stop=(c == KD - 1))
                    ins.then_inc(s_qk, 1)
                    for t in range(TT):
                        for c in range(KD):
                            ins = t_.matmul(work[s][:, 2, t * D:(t + 1) * D], hT[:, s, c, t * P:(t + 1) * P],
                                            wv_s[:, c], start=(c == 0), stop=(c == KD - 1))
                    ins.then_inc(s_v, 1)
                for s in range(NS):
                    pe.wait_ge(s_st[s], i * 192 + 192)
                    for g in range(NG):
                        k = s * NG + g
                        if k >= 2:
                            pe.wait_ge(s_max, i * NS * NG + k - 1)
                        else:
                            pe.wait_ge(s_p0, i * NS + k + 1)
                            pe.wait_ge(s_vr, i * NS + k + 1)
                        w = work[g % 2]
                        for j in range(HG // 2):
                            m2 = causal[:, :].unsqueeze(1).to_broadcast([P, 2, P])
                            t_.matmul(w[:, j, :].rearrange("p (h k) -> p h k", h=2)[:, :, P:T], ident_b[:, :], m2,
                                      start=True, stop=False, skip_group_check=True)
                            for hh in range(2):
                                hd = g * HG + 2 * j + hh
                                t_.matmul(w[:, j, hh * T:(hh + 1) * T], q_st[0:CR, s, hd, P:T], k_st[0:CR, s, hd],
                                          start=False, stop=(hh == 1), skip_group_check=True)
                        m4 = causal[:, :].unsqueeze(1).to_broadcast([P, HG, P])
                        t_.matmul(w[:, 2, :].rearrange("p (h k) -> p h k", h=HG), ident_b[:, :], m4,
                                  start=True, stop=False, skip_group_check=True)
                        for hh in range(HG):
                            hd = g * HG + hh
                            ins = t_.matmul(w[:, 2, hh * P:(hh + 1) * P], q_st[0:CR, s, hd, 0:P],
                                            k_st[0:CR, s, hd, 0:P], start=False, stop=(hh == HG - 1),
                                            skip_group_check=True)
                        ins.then_inc(s_s, 1)
                for s in range(NS):
                    pe.wait_ge(s_mp, i * NS + s + 1)
                    settled(pe)
                    for t in range(TT):
                        ins = t_.transpose(side[s][0:3 * H, t * P // 2:(t + 1) * P // 2].bitcast(BF16),
                                           nmax_p[:, s, t].rearrange("p a h -> p (a h)"), ident_b[:, :])
                    ins.then_inc(s_mt, 1)

                def logits_t(k):
                    s, g = k // NG, k % NG
                    if g == 0:
                        pe.wait_ge(s_mr[s], i * 48 + 48)
                    if k >= 2:
                        pe.wait_ge(s_exp, i * NS * NG + k - 1)
                    else:
                        pe.wait_ge(s_max, i * NS * NG + NS * NG)
                    w = work[k % 2]
                    for hh in range(HG):
                        hd = g * HG + hh
                        j, o = hh // 2, (hh % 2) * T
                        t_.matmul(w[:, j, o:o + T], k_st[0:CR + 3, s, hd, 0:P], q_st[0:CR + 3, s, hd],
                                  start=True, stop=True)
                        ins = t_.matmul(w[:, 2, hh * P:(hh + 1) * P], k_st[0:CR + 3, s, hd, P:T],
                                        q_st[0:CR + 3, s, hd, P:T], start=True, stop=True)
                    ins.then_inc(s_lt, 1)

                def weigh_v(k):
                    s, g = k // NG, k % NG
                    pe.wait_ge(s_msk, i * NS * NG + k + 1)
                    half, c0 = g // 2, (g % 2) * T
                    if g % 2 == 0:
                        if k >= NG:
                            pe.wait_ge(s_on, i * 2 * NS + k // 2 - 1)
                        elif k == 2:
                            pe.wait_ge(s_ms, i * NS + NS)
                    for hh in range(HG):
                        hd = g * HG + hh
                        o = side[half][32 * hh:32 * hh + 32, :]
                        t_.matmul(o[:, c0:c0 + T], v_s[:, s, 0, hd], pexp[:, k % 2, hh * T:(hh + 1) * T],
                                  start=True, stop=False)
                        ins = t_.matmul(o[:, c0 + P:c0 + T], v_s[:, s, 1, hd],
                                        pexp[:, k % 2, HG * T + hh * P:HG * T + (hh + 1) * P],
                                        start=False, stop=True)
                    ins.then_inc(s_pv, 1)

                logits_t(0)
                for k in range(1, NS * NG):
                    logits_t(k)
                    weigh_v(k - 1)
                weigh_v(NS * NG - 1)
                for s in range(NS):
                    pe.wait_ge(s_on, i * 2 * NS + 2 * NS - (NS - 1 - s))
                    for t in range(TT):
                        for g in range(NG):
                            ins = t_.matmul(side[s][:, t * D:(t + 1) * D], oT[:, s, g, t * P:(t + 1) * P],
                                            wo_s[:, g], start=(g == 0), stop=(g == NG - 1))
                    ins.then_inc(s_wo, 1)
                ffn(i, 1)


def kernel(**inputs):
    import numpy as np
    import concourse.bacc as bacc
    from concourse.bass_utils import run_bass_kernel_spmd

    a = {k.replace("L0_attn_a_", "a_").replace("L0_attn_b_", "b_").replace("L0_ffn_", "f_"): np.asarray(v)
         for k, v in inputs.items()}
    heads = lambda w: w.reshape(2, 8, 16, 256).transpose(3, 0, 2, 1).reshape(256, 256)
    bias = lambda b: b.reshape(2, 8, 16).transpose(2, 1, 0).reshape(128, 2)
    laid = {
        "x": a["a_x"],
        "nu": np.tile(a["a_nu_log"], 4).reshape(128, 1), "theta": np.tile(a["a_theta_log"], 4).reshape(128, 1),
        "b_re": a["a_B_re"].T, "b_im": a["a_B_im"].T, "c_re": a["a_C_re"].T, "c_im": a["a_C_im"].T,
        "d": a["a_D"],
        "wq": heads(a["b_Wq"]), "bq": bias(a["b_bq"]), "wk": heads(a["b_Wk"]), "bk": bias(a["b_bk"]),
        "wv": a["b_Wv"].T, "bv": a["b_bv"], "wo": a["b_Wo"].T, "bo": a["b_bo"],
        "w_up": a["f_W_up"].T, "w_gate": a["f_W_gate"].T, "w_down": a["f_W_down"].T,
    }
    nc = bacc.Bacc("TRN2", target_bir_lowering=False, num_devices=1)
    arrays, args = {}, []
    for name, v in laid.items():
        v = np.ascontiguousarray(v)
        arrays[f"in_{name}"] = v
        args.append(nc.dram_tensor(f"in_{name}", v.shape, mybir.dt.from_np(v.dtype), kind="ExternalInput").ap())
    args.append(nc.dram_tensor("out_0", a["a_x"].shape, mybir.dt.float32, kind="ExternalOutput").ap())
    hybrid_block_kernel(nc, *args)
    r = run_bass_kernel_spmd(nc, [arrays], core_ids=[0])
    return r.results[0]["out_0"]
```

```python
import concourse.bass as bass
from concourse import mybir
from contextlib import ExitStack


def hybrid_block_kernel(nc, x, nu, theta, b_re, b_im, c_re, c_im, dvec,
                        wq, bq, wk, bk, wv, bv, wo, bo, w_up, w_gate, w_down, out):
    F32, F16, BF16, I32 = mybir.dt.float32, mybir.dt.float16, mybir.dt.bfloat16, mybir.dt.int32
    ALU, ACT, AX = mybir.AluOpType, mybir.ActivationFunctionType, mybir.AxisListType

    P = 128
    B, T, D = x.shape
    TT = T // P
    KD = D // P
    FE = w_up.shape[1]
    NE = FE // P
    H = 16
    HD = D // H
    HT = P // HD
    NST = b_re.shape[1]
    HG = 4
    NG = H // HG
    SLOT = HG * T + HG * P
    CR = 6 * HD
    LN_EPS, Q_EPS = 1e-5, 1e-8
    UP = 2.0 ** 11
    KHID = 0.25 / (UP * UP)
    NEG = -1.0e30
    ROUND = 12582912.0
    ROUND16 = 192.0
    TWO_PI = 6.283185
    Q_PART = (0, 1, 2, 0, 1, 0)
    K_PART = (0, 0, 0, 1, 1, 2)
    NORM_SCALE = (1.0, UP, 1.0, UP)

    ctx = ExitStack()
    with ctx:
        def sb(name, shape, dt):
            return ctx.enter_context(nc.sbuf_tensor(name, shape, dt))

        def sem(name):
            return ctx.enter_context(nc.semaphore(name))

        wu_q = sb("wu_q", [P, KD, FE], F16)
        wg_q = sb("wg_q", [P, KD, FE], F16)
        wd_q = sb("wd_q", [P, NE, D], F16)
        wq_s = sb("wq_s", [P, KD, D], F32)
        wk_s = sb("wk_s", [P, KD, D], F32)
        wv_s = sb("wv_s", [P, KD, D], F32)
        wo_s = sb("wo_s", [P, KD, D], F32)
        bq_c = sb("bq_c", [P, KD], F32)
        bq4 = sb("bq4", [P, KD], F32)
        bk_c = sb("bk_c", [P, KD], F32)
        bv_b = sb("bv_b", [P, D], F32)
        bo_b = sb("bo_b", [P, D], F32)
        d_b = sb("d_b", [P, D], F32)
        bu_w = sb("bu_w", [P, KD, 2, 4 * NST], F32)
        c_w = sb("c_w", [P, D], F32)
        nu_c = sb("nu_c", [P, 1], F32)
        th_c = sb("th_c", [P, 1], F32)
        sgn = sb("sgn", [P, 1], F32)
        col = sb("col", [P, 16], F32)
        steps_i = sb("steps_i", [P, T], I32)
        steps = sb("steps", [P, T], F32)
        rot_in = sb("rot_in", [P, 2, T], F32)
        rot_out = sb("rot_out", [P, T], F32)
        decay = sb("decay", [P, T], F32)
        ident = sb("ident", [P, P], F32)
        ident_b = sb("ident_b", [P, P], BF16)
        causal = sb("causal", [P, P], BF16)
        ones = sb("ones", [P, P], F32)
        expo = sb("expo", [P, 2], F32)
        wsum = sb("wsum", [P, 4], F32)
        wscale = sb("wscale", [P, 4], F32)
        whalf = sb("whalf", [P, 2, 4], F32)
        k_tanh = sb("k_tanh", [P, 1], F32)
        k_down = sb("k_down", [P, 2], F32)

        w_f = [sb(f"w_f{m}", [P, KD * FE], F32) for m in range(3)]
        absw = sb("absw", [P, KD * FE], F32)
        below = sb("below", [P, KD * FE], F16)
        turn = sb("turn", [P, 3, T], F32)
        sin_t = sb("sin_t", [P, T], F32)
        cos_t = sb("cos_t", [P, T], F32)

        xin = sb("xin", [P, TT, D], F32)
        x1 = sb("x1", [P, TT, D], F32)
        x2 = sb("x2", [P, TT, D], F32)
        x2_held = sb("x2_held", [P, TT, D], F32)
        x2b = sb("x2b", [P, TT, D], F32)
        x3 = sb("x3", [P, TT, D], F32)
        x4 = sb("x4", [P, TT, D], F32)
        xd = sb("xd", [P, TT, D], F32)
        h = [sb(f"h{n}", [P, TT, D], F32) for n in range(4)]
        stats = sb("stats", [P, 4, TT, 6], F32)
        mv = sb("mv", [P, 4, TT, 2], F32)
        vs = sb("vs", [P, 4, TT], F32)
        rstd = sb("rstd", [P, 4, TT], F32)
        hT = {n: sb(f"h{n}T", [P, KD, T], F32) for n in (0, 2)}
        hT_hi = {n: sb(f"h{n}T_hi", [P, KD, T], F16) for n in (1, 3)}
        hT_lo = {n: sb(f"h{n}T_lo", [P, KD, T], F16) for n in (1, 3)}
        rec = sb("rec", [P, 4, T], F32)
        rec_o = sb("rec_o", [P, T], F32)
        th = sb("th", [P, 3, T], F32)
        up1 = sb("up1", [P, 2, T], F32)
        hid = sb("hid", [P, 2, 2, T], F32)
        hid_hi = sb("hid_hi", [P, NE, T], F16)
        hid_lo = sb("hid_lo", [P, NE, T], F16)
        qk = sb("qk", [P, 2 * KD, T], F32)
        qk_r = sb("qk_r", [P, 2 * KD, T], F32)
        parts = sb("parts", [P, 3, 2 * KD, T], BF16)
        q_st = sb("q_st", [P, H, T], BF16)
        k_st = sb("k_st", [P, H, T], BF16)
        v_s = sb("v_s", [P, TT, H, 2 * HD], F32)
        nmax = sb("nmax", [P, TT, H], F32)
        nmax_r = sb("nmax_r", [P, TT, H], F32)
        nmax_p = sb("nmax_p", [P, TT, 3, H], BF16)
        nmax_t = sb("nmax_t", [3 * H, T], BF16)
        pexp = sb("pexp", [P, 2, SLOT], F32)
        uT = sb("uT", [P, 2, 2 * T], F32)
        rsum = sb("rsum", [P, TT, H], F32)
        o = sb("o", [P, TT, D], F32)
        oT = sb("oT", [P, KD, T], F32)

        scratch = nc.dram_tensor("qk_parts", (3, 2 * KD, P, T), BF16, kind="Internal").ap()

        ffn_ps = [ctx.enter_context(nc.psum_tensor(f"ffn_ps{n}", [P, 2, T], F32)) for n in range(3)]
        att_ps = ctx.enter_context(nc.psum_tensor("att_ps", [P, 3, 512], F32))
        att_side = ctx.enter_context(nc.psum_tensor("att_side", [P, 512], F32))
        ffn_side = ctx.enter_context(nc.psum_tensor("ffn_side", [P, 512], F32))
        side = [att_side, ffn_side, att_side, ffn_side]

        s_nu = sem("nu_theta_in")
        s_w = sem("weights_in")
        s_wf = [sem(f"ffn_weight{m}_in") for m in range(3)]
        s_const = sem("constants_ready")
        s_abs = sem("weight_abs_sums")
        s_tot = sem("weight_totals")
        s_quant = sem("weights_quantised")
        s_gam = sem("gamma_ready")
        s_mag = sem("mag_exponent_ready")
        s_theta = sem("exponentials_ready")
        s_phase = sem("phases_ready")
        s_sin = sem("sines_ready")
        s_tab = sem("ffn_scales_ready")
        s_bq = sem("query_bias_ready")
        s_omg = sem("gamma_square_ready")
        s_prep = sem("dve_preparation_steps")
        s_pprep = sem("pool_preparation_steps")

        s_x = sem("x_in")
        s_st0 = [sem(f"stats{n}_ready") for n in range(4)]
        s_mv = [sem(f"moments{n}_ready") for n in range(4)]
        s_vs = [sem(f"variance{n}_ready") for n in range(4)]
        s_rstd = [sem(f"rstd{n}_ready") for n in range(4)]
        s_h = [sem(f"norm{n}_ready") for n in range(4)]
        s_tr = [sem(f"norm{n}_transposed") for n in range(4)]
        s_hi = [sem(f"norm{n}T_copied") for n in range(4)]
        s_lo = {n: sem(f"norm{n}T_low_ready") for n in (1, 3)}
        s_xd = sem("skip_ready")
        s_dh = sem("scaled_norm_ready")
        s_bu = sem("input_maps_done")
        s_rot = sem("inputs_rotated")
        s_rec = sem("recurrence_steps")
        s_y = sem("recurrence_out_done")
        s_x1 = sem("x1_ready")
        s_ug = [sem(f"up_gate{f}_done") for f in range(2)]
        s_th = [sem(f"tanh{f}_done") for f in range(2)]
        s_up1 = [sem(f"gated_up{f}_ready") for f in range(2)]
        s_hid = [sem(f"hidden{f}_ready") for f in range(2)]
        s_hhi = [sem(f"hidden{f}_high_ready") for f in range(2)]
        s_hlo = [sem(f"hidden{f}_low_ready") for f in range(2)]
        s_dn = [sem(f"down{f}_done") for f in range(2)]
        s_res = [sem(f"ffn{f}_residual_ready") for f in range(2)]
        s_qk = sem("qk_done")
        s_v = sem("v_done")
        s_vr = sem("v_ready")
        s_qkb = sem("biased_qk_ready")
        s_p0, s_r1, s_p1, s_p2 = sem("part0_ready"), sem("rest1_ready"), sem("part1_ready"), sem("part2_ready")
        s_sw = sem("scratch_written")
        s_st = sem("stacks_in")
        s_s = sem("scores_done")
        s_max = sem("max_done")
        s_mp = sem("max_part_steps")
        s_mt = sem("max_transposed")
        s_ms = sem("max_rows_ready")
        s_mr = sem("max_rows_in")
        s_lt = sem("logits_t_done")
        s_exp = sem("exp_done")
        s_msk = sem("masked")
        s_pv = sem("pv_done")
        s_uc = sem("heads_copied")
        s_ut = sem("heads_turned")
        s_rs = sem("row_sums_inverted")
        s_on = sem("heads_normalised")
        s_ot = sem("attention_turned_back")
        s_oT = sem("attention_ready")
        s_x2h = sem("x2_copied")
        s_xbo = sem("bias_added")
        s_wo = sem("wo_done")
        s_x3 = sem("x3_ready")
        s_out = sem("out_written")

        N2 = 2 * NG
        small = [
            (d_b[:, :], dvec.partition_broadcast(P)),
            (c_w[0:NST, :], c_re), (c_w[NST:2 * NST, :], c_im),
            (c_w[2 * NST:3 * NST, :], c_im), (c_w[3 * NST:4 * NST, :], c_re),
            (bq_c[:, :], bq), (bk_c[:, :], bk),
            (bv_b[:, :], bv.partition_broadcast(P)), (bo_b[:, :], bo.partition_broadcast(P)),
            (wq_s[:, :, :], wq.rearrange("(k p) o -> p k o", p=P)),
            (wk_s[:, :, :], wk.rearrange("(k p) o -> p k o", p=P)),
            (wv_s[:, :, :], wv.rearrange("(k p) o -> p k o", p=P)),
            (wo_s[:, :, :], wo.rearrange("(k p) o -> p k o", p=P)),
        ]
        for half in range(2):
            for m, src in enumerate((b_re, b_im, b_im, b_re)):
                c0 = 2 * NST * half + NST * (m % 2)
                small.insert(0, (bu_w[:, :, m // 2, c0:c0 + NST], src.rearrange("(k p) n -> p k n", p=P)))

        def settled(eng):
            eng.nop(nofuse=True)

        block = ctx.enter_context(nc.Block())

        @block.sync
        def _(sp):
            x_v = x.rearrange("b (t p) d -> b p t d", p=P)
            o_v = out.rearrange("b (t p) d -> b p t d", p=P)
            sp.dma_start(nu_c[:, :], nu).then_inc(s_nu, 16)
            sp.dma_start(th_c[:, :], theta).then_inc(s_nu, 16)
            sp.dma_start(xin[:, :, :], x_v[0]).then_inc(s_x, 16)
            for dst, src in small[:13]:
                sp.dma_start(dst, src).then_inc(s_w, 16)
            for m, w in enumerate((w_up, w_gate, w_down)):
                sp.dma_start(w_f[m][:, :].rearrange("p (k e) -> p k e", e=w.shape[1]),
                             w.rearrange("(k p) e -> p k e", p=P)).then_inc(s_wf[m], 16)
            for dst, src in small[13:]:
                sp.dma_start(dst, src).then_inc(s_w, 16)

            def load_x(q):
                sp.wait_ge(s_xd, q * TT)
                sp.wait_ge(s_h[0], q)
                sp.dma_start(xin[:, :, :], x_v[q]).then_inc(s_x, 16)

            def write_parts(q):
                sp.wait_ge(s_p2, q + 1)
                sp.dma_start(scratch.rearrange("a k p t -> p (a k) t"),
                             parts[:, :, :, :].rearrange("p a k t -> p (a k) t")).then_inc(s_sw, 16)

            def stacks(q):
                sp.wait_ge(s_sw, q * 16 + 16)
                for c in range(6):
                    for stack, part, base in ((q_st, Q_PART[c], 0), (k_st, K_PART[c], KD)):
                        sp.dma_start(stack[c * HD:(c + 1) * HD].rearrange("i (k g) t -> i k (g t)", k=KD),
                                     scratch[part, base:base + KD].rearrange("k (i g) t -> i k (g t)", g=HT)
                                     ).then_inc(s_st, 16)

            def max_rows(q):
                sp.wait_ge(s_ms, q + 1)
                for a in range(3):
                    sp.dma_start(q_st[CR + a:CR + a + 1], nmax_t[a * H:(a + 1) * H]).then_inc(s_mr, 16)

            def store(q):
                sp.wait_ge(s_res[1], q + 1)
                sp.dma_start(o_v[q], x4[:, :, :]).then_inc(s_out, 16)

            def trip(b, att=True, qkv=True, load=True, ffn=True):
                if load:
                    load_x(b + 3)
                if att:
                    max_rows(b)
                if qkv:
                    write_parts(b + 1)
                if ffn:
                    store(b - 1)
                if qkv:
                    if att:
                        sp.wait_ge(s_lt, b * N2 + N2)
                        settled(sp)
                    if ffn:
                        sp.wait_ge(s_out, b * 16)
                    settled(sp)
                    stacks(b + 1)

            load_x(1)
            trip(-1, att=False, ffn=False)
            trip(0, ffn=False)
            with nc.sync.Fori(1, B - 3) as b:
                trip(b)
            for b in range(B - 3, B):
                trip(b, load=False, qkv=b + 1 < B)
            store(B - 1)
            sp.wait_ge(s_out, B * 16)

        @block.gpsimd
        def _(pool):
            g = nc.gpsimd
            n = [0]

            def link(ins):
                n[0] += 1
                ins.then_inc(s_pprep, 1)
                pool.wait_ge(s_pprep, n[0])

            g.iota(steps_i[:, :], pattern=[[1, T]], base=0, channel_multiplier=0)
            g.memset(expo[:, 0:1], -0.5)
            g.memset(expo[:, 1:2], 0.5)
            link(g.memset(ident[:, :], 0.0))
            g.affine_select(out=ident[:, :], in_=ident[:, :], compare_op=ALU.not_equal, fill=1.0, base=0,
                            pattern=[[-1, P]], channel_multiplier=1)
            g.tensor_copy(steps[:, :], steps_i[:, :]).then_inc(s_const, 1)

            def norm_rstd(n_, q):
                pool.wait_ge(s_mv[n_], q + 1)
                settled(pool)
                g.tensor_scalar(vs[:, n_], mv[:, n_, :, 1], LN_EPS, NORM_SCALE[n_] ** -2,
                                ALU.add, ALU.mult).then_inc(s_vs[n_], 1)
                pool.wait_ge(s_vs[n_], q + 1)
                g.tensor_tensor(rstd[:, n_], vs[:, n_], expo[:, 0:1].to_broadcast([P, TT]),
                                ALU.pow).then_inc(s_rstd[n_], 1)

            def skip(q):
                pool.wait_ge(s_h[0], q + 1)
                for t in range(TT):
                    g.tensor_tensor(xd[:, t], h[0][:, t], d_b[:, :], ALU.mult).then_inc(s_dh, 1)
                for t in range(TT):
                    pool.wait_ge(s_dh, q * TT + t + 1)
                    g.tensor_tensor(xd[:, t], xd[:, t], xin[:, t], ALU.add).then_inc(s_xd, 1)

            def hidden_low(f, q, u):
                pool.wait_ge(s_hhi[f], q * (NE // 2) + u + 1)
                g.tensor_tensor(hid_lo[:, 2 * u:2 * u + 2], hid[:, u % 2], hid_hi[:, 2 * u:2 * u + 2],
                                ALU.subtract).then_inc(s_hlo[f], 1)

            def hold(q):
                pool.wait_ge(s_res[0], q + 1)
                if not isinstance(q, int) or q > 0:
                    pool.wait_ge(s_xbo, q)
                settled(pool)
                g.tensor_copy(x2_held[:, :, :], x2[:, :, :]).then_inc(s_x2h, 1)

            def add_bias(q, first):
                pool.wait_ge(s_x2h, q + 1)
                if not first:
                    pool.wait_ge(s_x3, q)
                for t in range(TT):
                    ins = g.tensor_tensor(x2b[:, t], x2_held[:, t], bo_b[:, :], ALU.add)
                ins.then_inc(s_xbo, 1)

            def mask(q, k):
                v = pexp[:, k % 2]
                for m, blocks in enumerate((v[:, 0:HG * T].rearrange("p (h q) -> p h q", h=HG)[:, :, 0:P],
                                            v[:, HG * T:SLOT].rearrange("p (h q) -> p h q", h=HG))):
                    pool.wait_ge(s_exp, q * N2 + 2 * k + m + 1)
                    settled(pool)
                    g.affine_select(out=blocks, in_=blocks, compare_op=ALU.is_ge, fill=0.0, base=0,
                                    pattern=[[0, HG], [1, P]], channel_multiplier=-1).then_inc(s_msk, 1)

            norm_rstd(0, 0)
            g.memset(ones[:, :], 1.0)
            g.memset(ident_b[:, :], 0.0)
            link(g.memset(causal[:, :], 0.0))
            g.affine_select(out=ident_b[:, :], in_=ident_b[:, :], compare_op=ALU.not_equal, fill=1.0, base=0,
                            pattern=[[-1, P]], channel_multiplier=1)
            g.affine_select(out=causal[:, :], in_=causal[:, :], compare_op=ALU.is_ge, fill=NEG, base=0,
                            pattern=[[-1, P]], channel_multiplier=1).then_inc(s_const, 1)
            pool.wait_ge(s_omg, 1)
            g.tensor_tensor(col[:, 5:6], col[:, 4:5], expo[:, 1:2], ALU.pow).then_inc(s_gam, 1)
            pool.wait_ge(s_w, 16 * len(small))
            skip(0)
            g.memset(v_s[:, :, :, :], 1.0)
            g.memset(k_st[:, :, :], 1.0).then_inc(s_const, 1)
            norm_rstd(1, 0)
            norm_rstd(0, 1)
            for u in range(NE // 2):
                hidden_low(0, 0, u)

            def trip(b, att=True, qkv=True, rec=True, load=True, ffn=True):
                if qkv:
                    norm_rstd(2, b + 1)
                if rec:
                    skip(b + 2)
                if att:
                    add_bias(b, first=not ffn)
                if ffn:
                    hidden_low(1, b - 1, 0)
                if rec:
                    norm_rstd(1, b + 2)
                if qkv:
                    hold(b + 1)
                if ffn:
                    hidden_low(1, b - 1, 1)
                    hidden_low(1, b - 1, 2)
                    hidden_low(1, b - 1, 3)
                if att:
                    mask(b, 0)
                    mask(b, 1)
                if load:
                    norm_rstd(0, b + 3)
                if att:
                    mask(b, 2)
                    mask(b, 3)
                if rec:
                    for u in range(NE // 2):
                        hidden_low(0, b + 2, u)
                if att:
                    norm_rstd(3, b)

            trip(-1, att=False, ffn=False)
            trip(0, ffn=False)
            with nc.gpsimd.Fori(1, B - 3) as b:
                trip(b)
            trip(B - 3, load=False)
            trip(B - 2, load=False, rec=False)
            trip(B - 1, load=False, rec=False, qkv=False)
            for u in range(NE // 2):
                hidden_low(1, B - 1, u)

        @block.scalar
        def _(act):
            a = nc.scalar

            def copy_hT(n, q):
                act.wait_ge(s_tr[n], q + 1)
                dst = hT[n] if n in hT else hT_hi[n]
                a.copy(dst[:, :, :], side[n][:, :].rearrange("p (k t) -> p k t", k=KD)).then_inc(s_hi[n], 1)

            def tanh(f, q, e):
                act.wait_ge(s_ug[f], q * NE + e + 1)
                if e >= 3:
                    act.wait_ge(s_up1[f], q * NE + e - 2)
                a.activation(th[:, e % 3], ffn_ps[e % 3][:, 0], ACT.Tanh, scale=k_tanh[:, 0:1]).then_inc(s_th[f], 1)

            def high(f, q, u):
                act.wait_ge(s_hid[f], q * NE + 2 * u + 2)
                a.copy(hid_hi[:, 2 * u:2 * u + 2], hid[:, u % 2]).then_inc(s_hhi[f], 1)

            def swiglu(f, q, es):
                for e in es:
                    tanh(f, q, e)
                    if e % 2 == 1 and e >= 3:
                        high(f, q, e // 2 - 1)
                if es[-1] == NE - 1:
                    high(f, q, NE // 2 - 1)

            def split_qk(q):
                act.wait_ge(s_qk, q + 1)
                for t in range(KD):
                    a.activation(qk[:, t], att_ps[:, 0, t * T:(t + 1) * T], ACT.Identity,
                                 bias=bq4[:, t:t + 1], scale=HD ** -0.5)
                for t in range(KD):
                    ins = a.activation(qk[:, KD + t], att_ps[:, 1, t * T:(t + 1) * T], ACT.Identity,
                                       bias=bk_c[:, t:t + 1])
                ins.then_inc(s_qkb, 1)
                act.wait_ge(s_qkb, q + 1)
                a.copy(parts[:, 0], qk[:, :, :]).then_inc(s_p0, 1)

            def part1(q):
                act.wait_ge(s_r1, q + 1)
                a.copy(parts[:, 1], qk_r[:, :, :]).then_inc(s_p1, 1)

            def max_turned(q):
                act.wait_ge(s_mt, q + 1)
                a.copy(nmax_t[:, :], att_side[0:3 * H, 0:P].bitcast(BF16)).then_inc(s_ms, 1)

            def exp(q, k):
                if k >= 2:
                    act.wait_ge(s_pv, q * NG + k - 1)
                for m, (c0, c1, src) in enumerate((
                        (0, HG * T, att_ps[:, 0:2, :].rearrange("p a b -> p (a b)")),
                        (HG * T, SLOT, att_ps[:, 2, :]))):
                    act.wait_ge(s_lt, q * N2 + 2 * k + m + 1)
                    a.activation(pexp[:, k % 2, c0:c1], src, ACT.Exp).then_inc(s_exp, 1)

            def copy_heads(q, half):
                act.wait_ge(s_pv, q * NG + 2 * half + 2)
                a.copy(uT[:, half], att_side[:, :]).then_inc(s_uc, 1)

            def copy_oT(q):
                act.wait_ge(s_ot, q + 1)
                a.copy(oT[:, :, :], att_ps[:, 2, :].rearrange("p (k t) -> p k t", k=KD)).then_inc(s_oT, 1)

            act.wait_ge(s_nu, 32)
            a.activation(col[:, 0:1], nu_c[:, :], ACT.Exp)
            a.activation(col[:, 1:2], th_c[:, :], ACT.Exp).then_inc(s_theta, 1)
            act.wait_ge(s_mag, 1)
            a.activation(col[:, 3:4], col[:, 2:3], ACT.Exp).then_inc(s_theta, 1)
            act.wait_ge(s_phase, 1)
            a.activation(sin_t[:, :], turn[:, 0], ACT.Sin, scale=TWO_PI)
            a.activation(cos_t[:, :], turn[:, 1], ACT.Sin, scale=TWO_PI).then_inc(s_sin, 1)
            copy_hT(0, 0)
            for m in range(3):
                act.wait_ge(s_wf[m], 16)
                if m:
                    act.wait_ge(s_abs, m)
                a.activation(absw[:, :], w_f[m][:, :], ACT.Abs, accum_out=wsum[:, m:m + 1]).then_inc(s_abs, 1)
            act.wait_ge(s_w, 16 * len(small))
            a.activation(bq4[:, :], bq_c[:, :], ACT.Copy, scale=HD ** -0.5).then_inc(s_bq, 1)
            act.wait_ge(s_bq, 1)
            copy_hT(1, 0)
            act.wait_ge(s_tab, 1)
            swiglu(0, 0, range(NE))

            def trip(b, att=True, qkv=True, rec=True, ffn=True):
                if rec:
                    copy_hT(0, b + 2)
                if ffn:
                    copy_hT(3, b - 1)
                    swiglu(1, b - 1, (0, 1, 2, 3))
                if qkv:
                    copy_hT(2, b + 1)
                if ffn:
                    swiglu(1, b - 1, (4, 5))
                if rec:
                    copy_hT(1, b + 2)
                if ffn:
                    swiglu(1, b - 1, (6,))
                if att:
                    max_turned(b)
                if ffn:
                    swiglu(1, b - 1, (7,))
                if qkv:
                    split_qk(b + 1)
                if rec:
                    swiglu(0, b + 2, (0,))
                if att:
                    exp(b, 0)
                if qkv:
                    part1(b + 1)
                if att:
                    exp(b, 1)
                if rec:
                    swiglu(0, b + 2, (1,))
                if att:
                    exp(b, 2)
                    copy_heads(b, 0)
                if rec:
                    swiglu(0, b + 2, (2,))
                if att:
                    exp(b, 3)
                if rec:
                    if ffn:
                        act.wait_ge(s_dn[1], b)
                    swiglu(0, b + 2, (3,))
                if att:
                    copy_heads(b, 1)
                if rec:
                    swiglu(0, b + 2, (4, 5))
                if att:
                    copy_oT(b)
                if rec:
                    swiglu(0, b + 2, (6, 7))

            trip(-1, att=False, ffn=False)
            trip(0, ffn=False)
            with nc.scalar.Fori(1, B - 2) as b:
                trip(b)
            trip(B - 2, rec=False)
            trip(B - 1, rec=False, qkv=False)
            copy_hT(3, B - 1)
            swiglu(1, B - 1, range(NE))

        @block.vector
        def _(dve):
            v = nc.vector
            n = [0]

            def link(ins):
                n[0] += 1
                ins.then_inc(s_prep, 1)
                dve.wait_ge(s_prep, n[0])

            def moments(m, q, src):
                for t in range(TT):
                    ins = v.bn_stats(stats[:, m, t], src[:, t])
                ins.then_inc(s_st0[m], 1)
                dve.wait_ge(s_st0[m], q + 1)
                settled(dve)
                for t in range(TT):
                    ins = v.bn_aggr(mv[:, m, t], stats[:, m, t])
                ins.then_inc(s_mv[m], 1)

            def normalise(m, q, src):
                dve.wait_ge(s_rstd[m], q + 1)
                for t in range(TT):
                    ins = v.tensor_scalar(h[m][:, t], src[:, t], mv[:, m, t, 0:1], rstd[:, m, t:t + 1],
                                          ALU.subtract, ALU.mult)
                ins.then_inc(s_h[m], 1)

            def low(m, q):
                dve.wait_ge(s_hi[m], q + 1)
                v.tensor_tensor(hT_lo[m][:, :, :], side[m][:, :].rearrange("p (k t) -> p k t", k=KD),
                                hT_hi[m][:, :, :], ALU.subtract).then_inc(s_lo[m], 1)

            def recurrence(q):
                dve.wait_ge(s_bu, q + 1)
                v.tensor_tensor(rec[:, 0], att_side[:, 0:T], rot_in[:, 0], ALU.mult)
                v.tensor_tensor(rec[:, 1], att_side[:, T:2 * T], rot_in[:, 1], ALU.mult).then_inc(s_rot, 1)
                dve.wait_ge(s_rot, q * 2 + 1)
                v.tensor_tensor(rec[:, 2], rec[:, 0], rec[:, 1], ALU.add).then_inc(s_rot, 1)
                dve.wait_ge(s_rot, q * 2 + 2)
                v.tensor_tensor_scan(rec[:, 3], decay[:, :], rec[:, 2], 0.0, ALU.mult, ALU.add).then_inc(s_rec, 1)
                dve.wait_ge(s_rec, q * 2 + 1)
                v.tensor_tensor(rec_o[:, :], rec[:, 3], rot_out[:, :], ALU.mult).then_inc(s_rec, 1)

            def residual1(q):
                dve.wait_ge(s_xd, q * TT + TT)
                dve.wait_ge(s_y, q + 1)
                v.tensor_tensor(x1[:, :, :].rearrange("p t d -> p (t d)"), att_side[:, :],
                                xd[:, :, :].rearrange("p t d -> p (t d)"), ALU.add).then_inc(s_x1, 1)
                dve.wait_ge(s_x1, q + 1)

            def hidden(f, q, es):
                for e in es:
                    dve.wait_ge(s_th[f], q * NE + e + 1)
                    if e >= 4 and e % 2 == 0:
                        dve.wait_ge(s_hlo[f], q * (NE // 2) + e // 2 - 1)
                    v.scalar_tensor_tensor(up1[:, e % 2], th[:, e % 3], 1.0, ffn_ps[e % 3][:, 0],
                                           ALU.add, ALU.mult).then_inc(s_up1[f], 1)
                    dve.wait_ge(s_up1[f], q * NE + e + 1)
                    v.scalar_tensor_tensor(hid[:, (e // 2) % 2, e % 2], up1[:, e % 2], KHID, ffn_ps[e % 3][:, 1],
                                           ALU.mult, ALU.mult).then_inc(s_hid[f], 1)

            def ffn_residual(f, q, src, dst):
                dve.wait_ge(s_dn[f], q + 1)
                v.scalar_tensor_tensor(dst[:, :, :].rearrange("p t d -> p (t d)"), ffn_side[:, :], k_down[:, 1:2],
                                       src[:, :, :].rearrange("p t d -> p (t d)"),
                                       ALU.mult, ALU.add).then_inc(s_res[f], 1)

            def take_v(q):
                dve.wait_ge(s_v, q + 1)
                for t in range(TT):
                    ins = v.tensor_tensor(v_s[:, t, :, 0:HD],
                                          att_ps[:, 2, t * D:(t + 1) * D].rearrange("p (h d) -> p h d", h=H),
                                          bv_b[:, :].rearrange("p (h d) -> p h d", h=H), ALU.add)
                ins.then_inc(s_vr, 1)

            def rest1(q):
                dve.wait_ge(s_p0, q + 1)
                v.tensor_tensor(qk_r[:, :, :], qk[:, :, :], parts[:, 0], ALU.subtract).then_inc(s_r1, 1)

            def part2(q):
                dve.wait_ge(s_p1, q + 1)
                v.tensor_tensor(parts[:, 2], qk_r[:, :, :], parts[:, 1], ALU.subtract).then_inc(s_p2, 1)

            def row_max(q, g):
                hs = slice(g * HG, (g + 1) * HG)
                dve.wait_ge(s_s, q * N2 + 2 * g + 1)
                v.tensor_reduce(nmax[:, 1, hs], att_ps[:, 0:2, :].rearrange("p a (h k) -> p (a h) k", k=T), AX.X,
                                ALU.max, negate=True).then_inc(s_max, 1)
                dve.wait_ge(s_s, q * N2 + 2 * g + 2)
                v.tensor_reduce(nmax[:, 0, hs], att_ps[:, 2, :].rearrange("p (h k) -> p h k", k=P), AX.X,
                                ALU.max, negate=True).then_inc(s_max, 1)

            def max_parts(q):
                dve.wait_ge(s_max, q * N2 + N2)
                v.tensor_copy(nmax_p[:, :, 0], nmax[:, :, :]).then_inc(s_mp, 1)
                dve.wait_ge(s_mp, q * 4 + 1)
                v.tensor_tensor(nmax_r[:, :, :], nmax[:, :, :], nmax_p[:, :, 0], ALU.subtract).then_inc(s_mp, 1)
                dve.wait_ge(s_mp, q * 4 + 2)
                v.tensor_copy(nmax_p[:, :, 1], nmax_r[:, :, :]).then_inc(s_mp, 1)
                dve.wait_ge(s_mp, q * 4 + 3)
                v.tensor_tensor(nmax_p[:, :, 2], nmax_r[:, :, :], nmax_p[:, :, 1], ALU.subtract).then_inc(s_mp, 1)

            def normalise_heads(q, half):
                dve.wait_ge(s_ut, q * 2 + half + 1)
                u = att_ps[:, half, :].rearrange("p (t h e) -> p t h e", t=TT, e=2 * HD)
                hs = slice(half * H // 2, (half + 1) * H // 2)
                v.reciprocal(rsum[:, :, hs], u[:, :, :, HD]).then_inc(s_rs, 1)
                dve.wait_ge(s_rs, q * 2 + half + 1)
                for t in range(TT):
                    ins = v.tensor_tensor(o[:, t].rearrange("p (h d) -> p h d", h=H)[:, hs], u[:, t, :, 0:HD],
                                          rsum[:, t, hs].unsqueeze(2).to_broadcast([P, H // 2, HD]), ALU.mult)
                ins.then_inc(s_on, 1)

            def residual3(q):
                dve.wait_ge(s_wo, q + 1)
                dve.wait_ge(s_xbo, q + 1)
                v.tensor_tensor(x3[:, :, :].rearrange("p t d -> p (t d)"), att_side[:, :],
                                x2b[:, :, :].rearrange("p t d -> p (t d)"), ALU.add).then_inc(s_x3, 1)
                dve.wait_ge(s_x3, q + 1)

            for s in range(2):
                v.memset(sgn[2 * NST * s:2 * NST * s + NST, :], 1.0)
                v.memset(sgn[2 * NST * s + NST:2 * NST * (s + 1), :], -1.0)
            dve.wait_ge(s_theta, 1)
            v.tensor_scalar(col[:, 2:3], col[:, 0:1], -1.0, -1.0, ALU.mult, ALU.add).then_inc(s_mag, 1)
            link(v.tensor_scalar(col[:, 6:7], col[:, 1:2], 0.15915494309189535, None, ALU.mult))
            link(v.tensor_scalar(col[:, 7:8], col[:, 6:7], ROUND, ROUND, ALU.add, ALU.subtract))
            link(v.tensor_tensor(col[:, 8:9], col[:, 6:7], col[:, 7:8], ALU.subtract))
            link(v.tensor_scalar(col[:, 9:10], col[:, 8:9], ROUND16, ROUND16, ALU.add, ALU.subtract))
            link(v.tensor_tensor(col[:, 10:11], col[:, 8:9], col[:, 9:10], ALU.subtract))
            dve.wait_ge(s_const, 1)
            link(v.tensor_scalar(turn[:, 0], steps[:, :], col[:, 9:10], None, ALU.mult))
            link(v.tensor_scalar(turn[:, 1], turn[:, 0], ROUND, ROUND, ALU.add, ALU.subtract))
            link(v.tensor_tensor(turn[:, 2], turn[:, 0], turn[:, 1], ALU.subtract))
            link(v.scalar_tensor_tensor(turn[:, 1], steps[:, :], col[:, 10:11], turn[:, 2], ALU.mult, ALU.add))
            link(v.tensor_scalar(turn[:, 2], turn[:, 1], ROUND, ROUND, ALU.add, ALU.subtract))
            link(v.tensor_tensor(turn[:, 0], turn[:, 1], turn[:, 2], ALU.subtract))
            link(v.tensor_scalar(turn[:, 1], turn[:, 0], 0.25, None, ALU.add))
            link(v.tensor_scalar(turn[:, 2], turn[:, 1], ROUND, ROUND, ALU.add, ALU.subtract))
            v.tensor_tensor(turn[:, 1], turn[:, 1], turn[:, 2], ALU.subtract).then_inc(s_phase, 1)
            dve.wait_ge(s_x, 16)
            moments(0, 0, xin)
            dve.wait_ge(s_theta, 2)
            link(v.tensor_scalar(col[:, 11:12], col[:, 3:4], col[:, 3:4], -1.0, ALU.mult, ALU.mult))
            v.tensor_scalar(col[:, 4:5], col[:, 11:12], 1.0, 0.0, ALU.add, ALU.max).then_inc(s_omg, 1)
            v.tensor_scalar(decay[:, :], steps[:, :], 0.0, col[:, 3:4], ALU.mult, ALU.add)
            normalise(0, 0, xin)
            dve.wait_ge(s_gam, 1)
            link(v.tensor_tensor(col[:, 12:13], col[:, 5:6], sgn[:, :], ALU.mult))
            dve.wait_ge(s_sin, 1)
            v.tensor_scalar(rot_in[:, 0], cos_t[:, :], col[:, 5:6], None, ALU.mult)
            v.tensor_scalar(rot_in[:, 1], sin_t[:, :], col[:, 12:13], None, ALU.mult)
            v.tensor_scalar(rot_out[0:2 * NST], cos_t[0:2 * NST, :], sgn[0:2 * NST, 0:1], None, ALU.mult)
            link(v.tensor_scalar(rot_out[2 * NST:], sin_t[2 * NST:, :], -1.0, None, ALU.mult))

            def quantise(m, q):
                dve.wait_ge(s_tot, m + 1)
                link(v.tensor_scalar(wscale[:, m:m + 1], ffn_ps[m][:, 0, 0:1], 1.0 / (D * FE), Q_EPS,
                                     ALU.mult, ALU.add))
                v.tensor_scalar(whalf[:, 0, m:m + 1], wscale[:, m:m + 1], 0.5, None, ALU.mult)
                link(v.tensor_scalar(whalf[:, 1, m:m + 1], wscale[:, m:m + 1], -0.5, None, ALU.mult))
                link(v.tensor_scalar(below[:, :], w_f[m][:, :], whalf[:, 1, m:m + 1], None, ALU.is_lt))
                v.scalar_tensor_tensor(q[:, :, :].rearrange("p k e -> p (k e)"), w_f[m][:, :],
                                       whalf[:, 0, m:m + 1], below[:, :], ALU.is_gt,
                                       ALU.subtract).then_inc(s_quant, 1)
                dve.wait_ge(s_quant, m + 1)

            recurrence(0)
            residual1(0)
            moments(1, 0, x1)
            quantise(0, wu_q)
            quantise(1, wg_q)
            v.tensor_scalar(k_tanh[:, :], wscale[:, 0:1], 0.5 / UP, None, ALU.mult).then_inc(s_tab, 1)
            link(v.tensor_scalar(k_down[:, 0:1], wscale[:, 0:1], wscale[:, 1:2], 2.0, ALU.mult, ALU.mult))
            normalise(1, 0, x1)
            low(1, 0)
            hidden(0, 0, range(2))
            quantise(2, wd_q)
            link(v.tensor_scalar(k_down[:, 1:2], k_down[:, 0:1], wscale[:, 2:3], None, ALU.mult))
            dve.wait_ge(s_x, 32)
            moments(0, 1, xin)
            hidden(0, 0, (2, 3))
            normalise(0, 1, xin)
            hidden(0, 0, range(4, NE))
            ffn_residual(0, 0, x1, x2)

            def trip(b, att=True, qkv=True, rec=True, load=True, ffn=True):
                if ffn:
                    low(3, b - 1)
                if qkv:
                    dve.wait_ge(s_res[0], b + 2)
                    moments(2, b + 1, x2)
                if rec:
                    recurrence(b + 2)
                if qkv:
                    normalise(2, b + 1, x2)
                if ffn:
                    hidden(1, b - 1, (0, 1))
                if att:
                    row_max(b, 0)
                if ffn:
                    hidden(1, b - 1, (2,))
                if rec:
                    residual1(b + 2)
                    moments(1, b + 2, x1)
                if att:
                    row_max(b, 1)
                if ffn:
                    hidden(1, b - 1, (3,))
                if att:
                    row_max(b, 2)
                if rec:
                    normalise(1, b + 2, x1)
                if ffn:
                    hidden(1, b - 1, (4,))
                if att:
                    row_max(b, 3)
                    max_parts(b)
                if ffn:
                    hidden(1, b - 1, (5,))
                if rec:
                    low(1, b + 2)
                if ffn:
                    hidden(1, b - 1, (6, 7))
                if qkv:
                    rest1(b + 1)
                if rec:
                    if ffn:
                        dve.wait_ge(s_hlo[1], b * (NE // 2))
                    hidden(0, b + 2, (0,))
                if ffn:
                    ffn_residual(1, b - 1, x3, x4)
                if qkv:
                    part2(b + 1)
                if load:
                    dve.wait_ge(s_x, b * 16 + 64)
                    moments(0, b + 3, xin)
                if rec:
                    hidden(0, b + 2, (1,))
                if load:
                    normalise(0, b + 3, xin)
                if rec:
                    hidden(0, b + 2, (2, 3, 4))
                if att:
                    normalise_heads(b, 0)
                    normalise_heads(b, 1)
                if qkv:
                    if att:
                        dve.wait_ge(s_pv, b * NG + NG)
                    take_v(b + 1)
                if rec:
                    hidden(0, b + 2, (5, 6, 7))
                if att:
                    residual3(b)
                    moments(3, b, x3)
                    normalise(3, b, x3)
                if rec:
                    dve.wait_ge(s_x2h, b + 2)
                    ffn_residual(0, b + 2, x1, x2)

            trip(-1, att=False, ffn=False)
            trip(0, ffn=False)
            with nc.vector.Fori(1, B - 3) as b:
                trip(b)
            trip(B - 3, load=False)
            trip(B - 2, load=False, rec=False)
            trip(B - 1, load=False, rec=False, qkv=False)
            low(3, B - 1)
            hidden(1, B - 1, range(NE))
            dve.wait_ge(s_out, (B - 1) * 16)
            ffn_residual(1, B - 1, x3, x4)

        @block.tensor
        def _(pe):
            t_ = nc.tensor

            def transpose_norm(m, q):
                pe.wait_ge(s_h[m], q + 1)
                for t in range(TT):
                    for c in range(KD):
                        ins = t_.transpose(side[m][:, c * T + t * P:c * T + (t + 1) * P],
                                           h[m][:, t, c * P:(c + 1) * P], ident[:, :])
                ins.then_inc(s_tr[m], 1)

            def input_maps(q):
                pe.wait_ge(s_hi[0], q + 1)
                for m in range(2):
                    for c in range(KD):
                        ins = t_.matmul(att_side[:, m * T:(m + 1) * T], bu_w[:, c, m], hT[0][:, c],
                                        start=(c == 0), stop=(c == KD - 1))
                ins.then_inc(s_bu, 1)

            def output_map(q):
                pe.wait_ge(s_rec, q * 2 + 2)
                for t in range(TT):
                    ins = t_.matmul(att_side[:, t * D:(t + 1) * D], rec_o[:, t * P:(t + 1) * P], c_w[:, :],
                                    start=True, stop=True)
                ins.then_inc(s_y, 1)

            def up_gate(f, q, es):
                m = 2 * f + 1
                if es[0] == 0:
                    pe.wait_ge(s_hi[m], q + 1)
                    pe.wait_ge(s_lo[m], q + 1)
                for e in es:
                    if e >= 3:
                        pe.wait_ge(s_hid[f], q * NE + e - 2)
                    for j, w in enumerate((wu_q, wg_q)):
                        for c in range(KD):
                            for part, src in enumerate((hT_hi[m], hT_lo[m])):
                                ins = t_.matmul(ffn_ps[e % 3][:, j], w[:, c, e * P:(e + 1) * P], src[:, c],
                                                start=(c == 0 and part == 0), stop=(c == KD - 1 and part == 1))
                    ins.then_inc(s_ug[f], 1)

            def down(f, q, t):
                for e in range(NE):
                    if t == 0 and e in (0, NE - 2):
                        pe.wait_ge(s_hlo[f], q * (NE // 2) + NE // 2 - (e == 0))
                    for part, src in enumerate((hid_hi, hid_lo)):
                        ins = t_.matmul(ffn_side[:, t * D:(t + 1) * D], src[:, e, t * P:(t + 1) * P], wd_q[:, e],
                                        start=(e == 0 and part == 0), stop=(e == NE - 1 and part == 1))
                if t == TT - 1:
                    ins.then_inc(s_dn[f], 1)

            def project_qk(q):
                pe.wait_ge(s_hi[2], q + 1)
                for m, w in ((0, wq_s), (1, wk_s)):
                    for t in range(KD):
                        for c in range(KD):
                            ins = t_.matmul(att_ps[:, m, t * T:(t + 1) * T], w[:, c, t * P:(t + 1) * P],
                                            hT[2][:, c], start=(c == 0), stop=(c == KD - 1))
                ins.then_inc(s_qk, 1)

            def project_v(q):
                for t in range(TT):
                    for c in range(KD):
                        ins = t_.matmul(att_ps[:, 2, t * D:(t + 1) * D], hT[2][:, c, t * P:(t + 1) * P],
                                        wv_s[:, c], start=(c == 0), stop=(c == KD - 1))
                ins.then_inc(s_v, 1)

            def scores(q, g):
                if g == 0:
                    pe.wait_ge(s_st, q * 192 + 192)
                    pe.wait_ge(s_vr, q + 1)
                else:
                    pe.wait_ge(s_max, q * N2 + 2 * g - 1)
                m2 = causal[:, :].unsqueeze(1).to_broadcast([P, 2, P])
                for j in range(HG // 2):
                    t_.matmul(att_ps[:, j, :].rearrange("p (h k) -> p h k", h=2)[:, :, P:T], ident_b[:, :], m2,
                              start=True, stop=False, skip_group_check=True)
                    for hh in range(2):
                        hd = g * HG + 2 * j + hh
                        ins = t_.matmul(att_ps[:, j, hh * T:(hh + 1) * T], q_st[0:CR, hd, P:T], k_st[0:CR, hd],
                                        start=False, stop=(hh == 1), skip_group_check=True)
                ins.then_inc(s_s, 1)
                if g:
                    pe.wait_ge(s_max, q * N2 + 2 * g)
                m4 = causal[:, :].unsqueeze(1).to_broadcast([P, HG, P])
                t_.matmul(att_ps[:, 2, :].rearrange("p (h k) -> p h k", h=HG), ident_b[:, :], m4,
                          start=True, stop=False, skip_group_check=True)
                for hh in range(HG):
                    hd = g * HG + hh
                    ins = t_.matmul(att_ps[:, 2, hh * P:(hh + 1) * P], q_st[0:CR, hd, 0:P], k_st[0:CR, hd, 0:P],
                                    start=False, stop=(hh == HG - 1), skip_group_check=True)
                ins.then_inc(s_s, 1)

            def turn_max(q):
                pe.wait_ge(s_mp, q * 4 + 4)
                settled(pe)
                for t in range(TT):
                    ins = t_.transpose(att_side[0:3 * H, t * P // 2:(t + 1) * P // 2].bitcast(BF16),
                                       nmax_p[:, t].rearrange("p a h -> p (a h)"), ident_b[:, :])
                ins.then_inc(s_mt, 1)

            def logits_t(q, g):
                if g == 0:
                    pe.wait_ge(s_mr, q * 48 + 48)
                    pe.wait_ge(s_max, q * N2 + N2)
                else:
                    pe.wait_ge(s_exp, q * N2 + 2 * g - 1)
                for hh in range(HG):
                    hd = g * HG + hh
                    ins = t_.matmul(att_ps[:, hh // 2, (hh % 2) * T:(hh % 2 + 1) * T], k_st[0:CR + 3, hd, 0:P],
                                    q_st[0:CR + 3, hd], start=True, stop=True)
                ins.then_inc(s_lt, 1)
                if g:
                    pe.wait_ge(s_exp, q * N2 + 2 * g)
                for hh in range(HG):
                    hd = g * HG + hh
                    ins = t_.matmul(att_ps[:, 2, hh * P:(hh + 1) * P], k_st[0:CR + 3, hd, P:T],
                                    q_st[0:CR + 3, hd, P:T], start=True, stop=True)
                ins.then_inc(s_lt, 1)

            def weigh_v(q, g):
                pe.wait_ge(s_msk, q * N2 + 2 * g + 2)
                if g == 2:
                    pe.wait_ge(s_uc, q * 2 + 1)
                c0 = (g % 2) * T
                for hh in range(HG):
                    hd = g * HG + hh
                    ps = att_side[32 * hh:32 * hh + 32, :]
                    t_.matmul(ps[:, c0:c0 + T], v_s[:, 0, hd], pexp[:, g % 2, hh * T:(hh + 1) * T],
                              start=True, stop=False)
                    ins = t_.matmul(ps[:, c0 + P:c0 + T], v_s[:, 1, hd],
                                    pexp[:, g % 2, HG * T + hh * P:HG * T + (hh + 1) * P],
                                    start=False, stop=True)
                ins.then_inc(s_pv, 1)

            def turn_heads(q, half):
                pe.wait_ge(s_uc, q * 2 + half + 1)
                pe.wait_ge(s_exp, q * N2 + N2)
                for t in range(TT):
                    for g in range(2):
                        c0 = t * 2 * P + g * P
                        ins = t_.transpose(att_ps[:, half, c0:c0 + P],
                                           uT[:, half, g * T + t * P:g * T + (t + 1) * P], ident[:, :])
                ins.then_inc(s_ut, 1)

            def turn_back(q):
                pe.wait_ge(s_on, q * 2 + 2)
                for t in range(TT):
                    for c in range(KD):
                        ins = t_.transpose(att_ps[:, 2, c * T + t * P:c * T + (t + 1) * P],
                                           o[:, t, c * P:(c + 1) * P], ident[:, :])
                ins.then_inc(s_ot, 1)

            def project_out(q):
                pe.wait_ge(s_oT, q + 1)
                for t in range(TT):
                    for c in range(KD):
                        ins = t_.matmul(att_side[:, t * D:(t + 1) * D], oT[:, c, t * P:(t + 1) * P], wo_s[:, c],
                                        start=(c == 0), stop=(c == KD - 1))
                ins.then_inc(s_wo, 1)

            pe.wait_ge(s_const, 1)
            transpose_norm(0, 0)
            pe.wait_ge(s_w, 16 * len(small))
            input_maps(0)
            pe.wait_ge(s_const, 2)
            for m in range(3):
                pe.wait_ge(s_abs, m + 1)
                t_.matmul(ffn_ps[m][:, 0, 0:1], ones[:, :], wsum[:, m:m + 1], start=True, stop=True).then_inc(s_tot, 1)
            output_map(0)
            transpose_norm(1, 0)
            pe.wait_ge(s_quant, 2)
            up_gate(0, 0, range(2))
            pe.wait_ge(s_quant, 3)
            up_gate(0, 0, range(2, NE))
            down(0, 0, 0)
            down(0, 0, 1)
            pe.wait_ge(s_const, 3)

            def trip(b, att=True, qkv=True, rec=True, ffn=True):
                if rec:
                    if ffn:
                        pe.wait_ge(s_x3, b)
                    transpose_norm(0, b + 2)
                if ffn:
                    if qkv:
                        pe.wait_ge(s_res[0], b + 2)
                    else:
                        pe.wait_ge(s_res[1], b - 1)
                    transpose_norm(3, b - 1)
                if rec:
                    input_maps(b + 2)
                if ffn:
                    up_gate(1, b - 1, (0, 1))
                if att:
                    scores(b, 0)
                if ffn:
                    up_gate(1, b - 1, (2,))
                if rec:
                    output_map(b + 2)
                if att:
                    scores(b, 1)
                if ffn:
                    up_gate(1, b - 1, (3,))
                if att:
                    scores(b, 2)
                if qkv:
                    if rec:
                        pe.wait_ge(s_x1, b + 3)
                    else:
                        pe.wait_ge(s_x3, b)
                    transpose_norm(2, b + 1)
                if ffn:
                    up_gate(1, b - 1, (4,))
                if att:
                    scores(b, 3)
                if ffn:
                    up_gate(1, b - 1, (5,))
                if rec:
                    if not ffn:
                        pe.wait_ge(s_res[0], b + 2)
                    transpose_norm(1, b + 2)
                if ffn:
                    up_gate(1, b - 1, (6,))
                if att:
                    if qkv:
                        pe.wait_ge(s_hi[2], b + 2)
                    else:
                        pe.wait_ge(s_x3, b)
                    turn_max(b)
                if ffn:
                    up_gate(1, b - 1, (7,))
                if qkv:
                    if att:
                        pe.wait_ge(s_max, b * N2 + N2)
                    project_qk(b + 1)
                if rec:
                    if ffn:
                        pe.wait_ge(s_hid[1], b * NE)
                    up_gate(0, b + 2, (0,))
                if ffn:
                    if rec:
                        pe.wait_ge(s_hi[1], b + 3)
                        pe.wait_ge(s_lo[1], b + 3)
                    down(1, b - 1, 0)
                if att:
                    if qkv:
                        pe.wait_ge(s_qkb, b + 2)
                    logits_t(b, 0)
                if ffn:
                    down(1, b - 1, 1)
                if att:
                    logits_t(b, 1)
                    weigh_v(b, 0)
                if rec:
                    up_gate(0, b + 2, (1,))
                if att:
                    logits_t(b, 2)
                    weigh_v(b, 1)
                if rec:
                    up_gate(0, b + 2, (2,))
                if att:
                    logits_t(b, 3)
                    weigh_v(b, 2)
                if rec:
                    up_gate(0, b + 2, (3,))
                if att:
                    weigh_v(b, 3)
                if rec:
                    up_gate(0, b + 2, (4,))
                if att:
                    turn_heads(b, 0)
                    turn_heads(b, 1)
                if qkv:
                    project_v(b + 1)
                if rec:
                    up_gate(0, b + 2, (5,))
                if att:
                    if qkv:
                        pe.wait_ge(s_vr, b + 2)
                    turn_back(b)
                if rec:
                    up_gate(0, b + 2, (6, 7))
                if att:
                    project_out(b)
                if rec:
                    if ffn:
                        pe.wait_ge(s_res[1], b)
                    down(0, b + 2, 0)
                    down(0, b + 2, 1)

            trip(-1, att=False, ffn=False)
            trip(0, ffn=False)
            with nc.tensor.Fori(1, B - 2) as b:
                trip(b)
            trip(B - 2, rec=False)
            trip(B - 1, rec=False, qkv=False)
            pe.wait_ge(s_res[1], B - 1)
            transpose_norm(3, B - 1)
            up_gate(1, B - 1, range(NE))
            down(1, B - 1, 0)
            down(1, B - 1, 1)


def kernel(**inputs):
    import numpy as np
    import concourse.bacc as bacc
    from concourse.bass_utils import run_bass_kernel_spmd

    a = {k.replace("L0_attn_a_", "a_").replace("L0_attn_b_", "b_").replace("L0_ffn_", "f_"): np.asarray(v)
         for k, v in inputs.items()}
    heads = lambda w: w.reshape(2, 8, 16, 256).transpose(3, 0, 2, 1).reshape(256, 256)
    bias = lambda b: b.reshape(2, 8, 16).transpose(2, 1, 0).reshape(128, 2)
    laid = {
        "x": a["a_x"],
        "nu": np.tile(a["a_nu_log"], 4).reshape(128, 1), "theta": np.tile(a["a_theta_log"], 4).reshape(128, 1),
        "b_re": a["a_B_re"].T, "b_im": a["a_B_im"].T, "c_re": a["a_C_re"].T, "c_im": a["a_C_im"].T,
        "d": a["a_D"],
        "wq": heads(a["b_Wq"]), "bq": bias(a["b_bq"]), "wk": heads(a["b_Wk"]), "bk": bias(a["b_bk"]),
        "wv": a["b_Wv"].T, "bv": a["b_bv"], "wo": a["b_Wo"].T, "bo": a["b_bo"],
        "w_up": a["f_W_up"].T, "w_gate": a["f_W_gate"].T, "w_down": a["f_W_down"].T,
    }
    nc = bacc.Bacc("TRN2", target_bir_lowering=False, num_devices=1)
    arrays, args = {}, []
    for name, v in laid.items():
        v = np.ascontiguousarray(v)
        arrays[f"in_{name}"] = v
        args.append(nc.dram_tensor(f"in_{name}", v.shape, mybir.dt.from_np(v.dtype), kind="ExternalInput").ap())
    args.append(nc.dram_tensor("out_0", a["a_x"].shape, mybir.dt.float32, kind="ExternalOutput").ap())
    hybrid_block_kernel(nc, *args)
    r = run_bass_kernel_spmd(nc, [arrays], core_ids=[0])
    return r.results[0]["out_0"]
```

```python
import concourse.bass as bass
from concourse import mybir
from contextlib import ExitStack


def hybrid_block_kernel(nc, x, nu, theta, b_maps, c_maps, dvec,
                        wq, bq, wk, bk, wv, bv, wo, bo, w_up, w_gate, w_down, out):
    F32, F16, BF16, I32 = mybir.dt.float32, mybir.dt.float16, mybir.dt.bfloat16, mybir.dt.int32
    ALU, ACT, AX = mybir.AluOpType, mybir.ActivationFunctionType, mybir.AxisListType

    P = 128
    B, T, D = x.shape
    TT = T // P
    KD = D // P
    FE = w_up.shape[1]
    NE = FE // P
    H = 16
    HD = D // H
    HT = P // HD
    NST = c_maps.shape[0] // 4
    HG = 4
    NG = H // HG
    SLOT = HG * T + HG * P
    CR = 6 * HD
    LN_EPS, Q_EPS = 1e-5, 1e-8
    UP = 2.0 ** 11
    KHID = 0.25 / (UP * UP)
    NEG = -1.0e30
    ROUND = 12582912.0
    ROUND16 = 192.0
    TWO_PI = 6.283185
    Q_PART = (0, 1, 2, 0, 0, 1)
    K_PART = (0, 1, 0, 1, 2, 0)
    NORM_SCALE = (1.0, UP, 1.0, UP)

    ctx = ExitStack()
    with ctx:
        def sb(name, shape, dt):
            return ctx.enter_context(nc.sbuf_tensor(name, shape, dt))

        def sem(name):
            return ctx.enter_context(nc.semaphore(name))

        wu_q = sb("wu_q", [P, KD, FE], F16)
        wg_q = sb("wg_q", [P, KD, FE], F16)
        wd_q = sb("wd_q", [P, NE, D], F16)
        wq_s = sb("wq_s", [P, KD, D], F32)
        wk_s = sb("wk_s", [P, KD, D], F32)
        wv_s = sb("wv_s", [P, KD, D], F32)
        wo_s = sb("wo_s", [P, KD, D], F32)
        bq_c = sb("bq_c", [P, KD], F32)
        bq4 = sb("bq4", [P, KD], F32)
        bk_c = sb("bk_c", [P, KD], F32)
        bv_b = sb("bv_b", [P, D], F32)
        bo_b = sb("bo_b", [P, D], F32)
        d_b = sb("d_b", [P, D], F32)
        bu_w = sb("bu_w", [P, KD, 2, 4 * NST], F32)
        c_w = sb("c_w", [P, D], F32)
        nu_c = sb("nu_c", [P, 1], F32)
        th_c = sb("th_c", [P, 1], F32)
        sgn = sb("sgn", [P, 1], F32)
        col = sb("col", [P, 16], F32)
        steps_i = sb("steps_i", [P, T], I32)
        steps = sb("steps", [P, T], F32)
        rot_in = sb("rot_in", [P, 2, T], F32)
        rot_out = sb("rot_out", [P, T], F32)
        decay = sb("decay", [P, T], F32)
        ident = sb("ident", [P, P], F32)
        ident_b = sb("ident_b", [P, P], BF16)
        causal = sb("causal", [P, P], BF16)
        ones = sb("ones", [P, P], F32)
        expo = sb("expo", [P, 2], F32)
        wsum = sb("wsum", [P, 4], F32)
        wscale = sb("wscale", [P, 4], F32)
        whalf = sb("whalf", [P, 2, 4], F32)
        k_tanh = sb("k_tanh", [P, 1], F32)
        k_down = sb("k_down", [P, 2], F32)

        w_f = [sb(f"w_f{m}", [P, KD * FE], F32) for m in range(3)]
        absw = sb("absw", [P, KD * FE], F32)
        below = sb("below", [P, KD * FE], F16)
        turn = sb("turn", [P, 3, T], F32)
        sin_t = sb("sin_t", [P, T], F32)
        cos_t = sb("cos_t", [P, T], F32)

        xin = sb("xin", [P, TT, D], F32)
        x1 = sb("x1", [P, TT, D], F32)
        x2 = sb("x2", [P, TT, D], F32)
        x2b = sb("x2b", [P, TT, D], F32)
        x3 = sb("x3", [P, TT, D], F32)
        x4 = sb("x4", [P, TT, D], F32)
        xd = sb("xd", [P, TT, D], F32)
        h = [sb(f"h{n}", [P, TT, D], F32) for n in range(4)]
        stats = sb("stats", [P, 4, TT, 6], F32)
        mv = sb("mv", [P, 4, TT, 2], F32)
        vs = sb("vs", [P, 4, TT], F32)
        rstd = sb("rstd", [P, 4, TT], F32)
        hT = {n: sb(f"h{n}T", [P, KD, T], F32) for n in (0, 2)}
        hT_hi = {n: sb(f"h{n}T_hi", [P, KD, T], F16) for n in (1, 3)}
        hT_lo = {n: sb(f"h{n}T_lo", [P, KD, T], F16) for n in (1, 3)}
        rec = sb("rec", [P, 4, T], F32)
        rec_o = sb("rec_o", [P, T], F32)
        th = sb("th", [P, 2, 2, T], F32)
        up1 = sb("up1", [P, 2, 2, T], F32)
        hid = sb("hid", [P, 2, 2, T], F32)
        hid_hi = sb("hid_hi", [P, NE, T], F16)
        hid_lo = sb("hid_lo", [P, NE, T], F16)
        qk = sb("qk", [P, 2 * KD, T], F32)
        qk_r = sb("qk_r", [P, 2 * KD, T], F32)
        parts = sb("parts", [P, 3, 2 * KD, T], BF16)
        q_st = sb("q_st", [P, H, T], BF16)
        k_st = sb("k_st", [P, H, T], BF16)
        v_s = sb("v_s", [P, TT, H, 2 * HD], F32)
        nmax = sb("nmax", [P, TT, H], F32)
        nmax_r = sb("nmax_r", [P, TT, H], F32)
        nmax_p = sb("nmax_p", [P, TT, 3, H], BF16)
        nmax_t = sb("nmax_t", [3 * H, T], BF16)
        pexp = sb("pexp", [P, 2, SLOT], F32)
        uT = sb("uT", [P, 2, 2 * T], F32)
        rsum = sb("rsum", [P, TT, H], F32)
        o = sb("o", [P, TT, D], F32)
        oT = sb("oT", [P, KD, T], F32)

        ffn_ps = [ctx.enter_context(nc.psum_tensor(f"ffn_ps{n}", [P, 2, T], F32)) for n in range(3)]
        att_ps = ctx.enter_context(nc.psum_tensor("att_ps", [P, 3, 512], F32))
        att_side = ctx.enter_context(nc.psum_tensor("att_side", [P, 512], F32))
        ffn_side = ctx.enter_context(nc.psum_tensor("ffn_side", [P, 512], F32))
        side = [att_side, ffn_side, ffn_side, ffn_side]

        s_nu = sem("nu_theta_in")
        s_maps = sem("recurrence_maps_in")
        s_w = sem("attention_weights_in")
        s_wf = [sem(f"ffn_weight{m}_in") for m in range(3)]
        s_const = sem("constants_ready")
        s_abs = sem("weight_abs_sums")
        s_tot = sem("weight_totals")
        s_quant = sem("weights_quantised")
        s_gam = sem("gamma_ready")
        s_mag = sem("mag_exponent_ready")
        s_theta = sem("exponentials_ready")
        s_phase = sem("phases_ready")
        s_sin = sem("sines_ready")
        s_tab = sem("ffn_scales_ready")
        s_bq = sem("query_bias_ready")
        s_omg = sem("gamma_square_ready")
        s_prep = sem("dve_preparation_steps")
        s_pprep = sem("pool_preparation_steps")

        s_x = sem("x_in")
        s_st0 = [sem(f"stats{n}_ready") for n in range(4)]
        s_mv = [sem(f"moments{n}_ready") for n in range(4)]
        s_vs = [sem(f"variance{n}_ready") for n in range(4)]
        s_rstd = [sem(f"rstd{n}_ready") for n in range(4)]
        s_h = [sem(f"norm{n}_ready") for n in range(4)]
        s_tr = [sem(f"norm{n}_transposed") for n in range(4)]
        s_hi = [sem(f"norm{n}T_copied") for n in range(4)]
        s_lo = {n: sem(f"norm{n}T_low_ready") for n in (1, 3)}
        s_xd = sem("skip_ready")
        s_dh = sem("scaled_norm_ready")
        s_bu = sem("input_maps_done")
        s_rot = sem("inputs_rotated")
        s_rec = sem("recurrence_steps")
        s_y = sem("recurrence_out_done")
        s_x1 = sem("x1_ready")
        s_ug = [sem(f"up_gate{f}_done") for f in range(2)]
        s_th = [sem(f"tanh{f}_done") for f in range(2)]
        s_up1 = [sem(f"gated_up{f}_ready") for f in range(2)]
        s_hid = [sem(f"hidden{f}_ready") for f in range(2)]
        s_hhi = [sem(f"hidden{f}_high_ready") for f in range(2)]
        s_hlo = [sem(f"hidden{f}_low_ready") for f in range(2)]
        s_dn = [sem(f"down{f}_done") for f in range(2)]
        s_res = [sem(f"ffn{f}_residual_ready") for f in range(2)]
        s_qk = sem("q_and_k_done")
        s_v = sem("v_done")
        s_vr = sem("v_ready")
        s_qkb = sem("biased_q_and_k_ready")
        s_p0, s_r1, s_p1, s_p2 = sem("part0_ready"), sem("rest1_ready"), sem("part1_ready"), sem("part2_ready")
        s_st = sem("stacks_in")
        s_s = sem("scores_done")
        s_max = sem("max_done")
        s_mp = sem("max_part_steps")
        s_mt = sem("max_transposed")
        s_ms = sem("max_rows_ready")
        s_mr = sem("max_rows_in")
        s_lt = sem("logits_t_done")
        s_exp = sem("exp_done")
        s_msk = sem("masked")
        s_pv = sem("pv_done")
        s_uc = sem("heads_copied")
        s_ut = sem("heads_turned")
        s_rs = sem("row_sums_inverted")
        s_on = sem("heads_normalised")
        s_ot = sem("attention_turned_back")
        s_oT = sem("attention_ready")
        s_xbo = sem("bias_added")
        s_wo = sem("wo_done")
        s_x3 = sem("x3_ready")
        s_out = sem("out_written")

        N2 = 2 * NG
        ST = 16 * (len(Q_PART) + len(K_PART))
        maps = [
            (bu_w[:, :, :, :], b_maps.rearrange("(k p) m n -> p k m n", p=P)),
            (c_w[:, :], c_maps),
            (d_b[:, :], dvec.partition_broadcast(P)),
        ]
        att_weights = [
            (bq_c[:, :], bq), (bk_c[:, :], bk),
            (bv_b[:, :], bv.partition_broadcast(P)), (bo_b[:, :], bo.partition_broadcast(P)),
            (wq_s[:, :, :], wq.rearrange("(k p) o -> p k o", p=P)),
            (wk_s[:, :, :], wk.rearrange("(k p) o -> p k o", p=P)),
            (wv_s[:, :, :], wv.rearrange("(k p) o -> p k o", p=P)),
            (wo_s[:, :, :], wo.rearrange("(k p) o -> p k o", p=P)),
        ]

        def settled(eng):
            eng.nop(nofuse=True)

        block = ctx.enter_context(nc.Block())

        @block.sync
        def _(sp):
            x_v = x.rearrange("b (t p) d -> b p t d", p=P)
            o_v = out.rearrange("b (t p) d -> b p t d", p=P)
            sp.dma_start(nu_c[:, :], nu).then_inc(s_nu, 16)
            sp.dma_start(th_c[:, :], theta).then_inc(s_nu, 16)
            sp.dma_start(xin[:, :, :], x_v[0]).then_inc(s_x, 16)
            for dst, src in maps:
                sp.dma_start(dst, src).then_inc(s_maps, 16)
            for m, w in enumerate((w_up, w_gate, w_down)):
                sp.dma_start(w_f[m][:, :].rearrange("p (k e) -> p k e", e=w.shape[1]),
                             w.rearrange("(k p) e -> p k e", p=P)).then_inc(s_wf[m], 16)
            for dst, src in att_weights:
                sp.dma_start(dst, src).then_inc(s_w, 16)

            def load_x(q):
                sp.wait_ge(s_xd, q * TT)
                sp.wait_ge(s_h[0], q)
                sp.dma_start(xin[:, :, :], x_v[q]).then_inc(s_x, 16)

            def stacks(q):
                for a, ready in enumerate((s_p0, s_p1, s_p2)):
                    sp.wait_ge(ready, q + 1)
                    for m, stack, part in ((0, q_st, Q_PART), (1, k_st, K_PART)):
                        for c in range(len(part)):
                            if part[c] == a:
                                rows = stack[c * HD:(c + 1) * HD].rearrange("i (g k) t -> i g (k t)", g=HT)
                                src = parts[:, a, m * KD:(m + 1) * KD, :].rearrange("p k t -> p (k t)")
                                sp.dma_start(rows, src).then_inc(s_st, 16)

            def max_rows(q):
                sp.wait_ge(s_ms, q + 1)
                for a in range(3):
                    sp.dma_start(q_st[CR + a:CR + a + 1], nmax_t[a * H:(a + 1) * H]).then_inc(s_mr, 16)

            def store(q):
                sp.wait_ge(s_res[1], q + 1)
                sp.dma_start(o_v[q], x4[:, :, :]).then_inc(s_out, 16)

            def first_trip():
                load_x(2)
                stacks(0)

            def second_trip():
                load_x(3)
                max_rows(0)
                sp.wait_ge(s_lt, N2)
                stacks(1)

            def trip(b, load=True):
                if load:
                    load_x(b + 3)
                max_rows(b)
                sp.wait_ge(s_lt, b * N2 + N2)
                settled(sp)
                stacks(b + 1)
                store(b - 1)
                sp.wait_ge(s_out, b * 16)
                settled(sp)

            def last_trip(b):
                max_rows(b)
                store(b - 1)
                sp.wait_ge(s_out, b * 16)

            load_x(1)
            first_trip()
            second_trip()
            with nc.sync.Fori(1, B - 3) as b:
                trip(b)
            trip(B - 3, load=False)
            trip(B - 2, load=False)
            last_trip(B - 1)
            store(B - 1)
            sp.wait_ge(s_out, B * 16)

        @block.gpsimd
        def _(pool):
            g = nc.gpsimd
            n = [0]

            def link(ins):
                n[0] += 1
                ins.then_inc(s_pprep, 1)
                pool.wait_ge(s_pprep, n[0])

            g.iota(steps_i[:, :], pattern=[[1, T]], base=0, channel_multiplier=0)
            g.memset(expo[:, 0:1], -0.5)
            g.memset(expo[:, 1:2], 0.5)
            link(g.memset(ident[:, :], 0.0))
            g.affine_select(out=ident[:, :], in_=ident[:, :], compare_op=ALU.not_equal, fill=1.0, base=0,
                            pattern=[[-1, P]], channel_multiplier=1)
            g.tensor_copy(steps[:, :], steps_i[:, :]).then_inc(s_const, 1)

            def norm_rstd(n_, q):
                pool.wait_ge(s_mv[n_], q + 1)
                settled(pool)
                g.tensor_scalar(vs[:, n_], mv[:, n_, :, 1], LN_EPS, NORM_SCALE[n_] ** -2,
                                ALU.add, ALU.mult).then_inc(s_vs[n_], 1)
                pool.wait_ge(s_vs[n_], q + 1)
                g.tensor_tensor(rstd[:, n_], vs[:, n_], expo[:, 0:1].to_broadcast([P, TT]),
                                ALU.pow).then_inc(s_rstd[n_], 1)

            def skip(q):
                pool.wait_ge(s_h[0], q + 1)
                for t in range(TT):
                    g.tensor_tensor(xd[:, t], h[0][:, t], d_b[:, :], ALU.mult).then_inc(s_dh, 1)
                for t in range(TT):
                    pool.wait_ge(s_dh, q * TT + t + 1)
                    g.tensor_tensor(xd[:, t], xd[:, t], xin[:, t], ALU.add).then_inc(s_xd, 1)

            def hidden_low(f, q, u):
                pool.wait_ge(s_hhi[f], q * (NE // 2) + u + 1)
                g.tensor_tensor(hid_lo[:, 2 * u:2 * u + 2], hid[:, u % 2], hid_hi[:, 2 * u:2 * u + 2],
                                ALU.subtract).then_inc(s_hlo[f], 1)

            def add_bias(q, first):
                pool.wait_ge(s_res[0], q + 1)
                if not first:
                    pool.wait_ge(s_x3, q)
                for t in range(TT):
                    ins = g.tensor_tensor(x2b[:, t], x2[:, t], bo_b[:, :], ALU.add)
                ins.then_inc(s_xbo, 1)

            def mask(q, k):
                v = pexp[:, k % 2]
                for m, blocks in enumerate((v[:, 0:HG * T].rearrange("p (h q) -> p h q", h=HG)[:, :, 0:P],
                                            v[:, HG * T:SLOT].rearrange("p (h q) -> p h q", h=HG))):
                    pool.wait_ge(s_exp, q * N2 + 2 * k + m + 1)
                    settled(pool)
                    g.affine_select(out=blocks, in_=blocks, compare_op=ALU.is_ge, fill=0.0, base=0,
                                    pattern=[[0, HG], [1, P]], channel_multiplier=-1).then_inc(s_msk, 1)

            norm_rstd(0, 0)
            g.memset(ones[:, :], 1.0)
            g.memset(ident_b[:, :], 0.0)
            link(g.memset(causal[:, :], 0.0))
            g.affine_select(out=ident_b[:, :], in_=ident_b[:, :], compare_op=ALU.not_equal, fill=1.0, base=0,
                            pattern=[[-1, P]], channel_multiplier=1)
            g.affine_select(out=causal[:, :], in_=causal[:, :], compare_op=ALU.is_ge, fill=NEG, base=0,
                            pattern=[[-1, P]], channel_multiplier=1).then_inc(s_const, 1)
            pool.wait_ge(s_omg, 1)
            g.tensor_tensor(col[:, 5:6], col[:, 4:5], expo[:, 1:2], ALU.pow).then_inc(s_gam, 1)
            pool.wait_ge(s_maps, 16 * len(maps))
            skip(0)
            g.memset(v_s[:, :, :, :], 1.0)
            g.memset(k_st[:, :, :], 1.0).then_inc(s_const, 1)
            norm_rstd(1, 0)
            norm_rstd(0, 1)
            hidden_low(0, 0, 0)

            def first_trip():
                for u in range(1, NE // 2):
                    hidden_low(0, 0, u)
                skip(1)
                norm_rstd(2, 0)
                norm_rstd(1, 1)
                norm_rstd(0, 2)
                hidden_low(0, 1, 0)

            def second_trip():
                add_bias(0, first=True)
                for u in range(1, NE // 2):
                    hidden_low(0, 1, u)
                skip(2)
                norm_rstd(2, 1)
                norm_rstd(1, 2)
                mask(0, 0)
                mask(0, 1)
                norm_rstd(0, 3)
                mask(0, 2)
                mask(0, 3)
                hidden_low(0, 2, 0)

            def trip(b, rec=True, load=True):
                add_bias(b, first=False)
                hidden_low(0, b + 1, 1)
                norm_rstd(3, b - 1)
                hidden_low(0, b + 1, 2)
                hidden_low(0, b + 1, 3)
                if rec:
                    skip(b + 2)
                norm_rstd(2, b + 1)
                if rec:
                    norm_rstd(1, b + 2)
                hidden_low(1, b - 1, 0)
                mask(b, 0)
                hidden_low(1, b - 1, 1)
                mask(b, 1)
                mask(b, 2)
                if load:
                    norm_rstd(0, b + 3)
                mask(b, 3)
                hidden_low(1, b - 1, 2)
                hidden_low(1, b - 1, 3)
                if rec:
                    hidden_low(0, b + 2, 0)

            def last_trip(b):
                norm_rstd(3, b - 1)
                add_bias(b, first=False)
                hidden_low(1, b - 1, 0)
                hidden_low(1, b - 1, 1)
                mask(b, 0)
                mask(b, 1)
                hidden_low(1, b - 1, 2)
                mask(b, 2)
                mask(b, 3)
                hidden_low(1, b - 1, 3)

            first_trip()
            second_trip()
            with nc.gpsimd.Fori(1, B - 3) as b:
                trip(b)
            trip(B - 3, load=False)
            trip(B - 2, load=False, rec=False)
            last_trip(B - 1)
            norm_rstd(3, B - 1)
            for u in range(NE // 2):
                hidden_low(1, B - 1, u)

        @block.scalar
        def _(act):
            a = nc.scalar

            def copy_hT(n, q):
                act.wait_ge(s_tr[n], q + 1)
                dst = hT[n] if n in hT else hT_hi[n]
                a.copy(dst[:, :, :], side[n][:, :].rearrange("p (k t) -> p k t", k=KD)).then_inc(s_hi[n], 1)

            def tanh(f, q, u):
                act.wait_ge(s_ug[f], q * NE + 2 * u + 1)
                if u >= 2:
                    act.wait_ge(s_up1[f], q * (NE // 2) + u - 1)
                a.activation(th[:, u % 2], ffn_ps[2 * u % 3][:, :], ACT.Tanh,
                             scale=k_tanh[:, 0:1]).then_inc(s_th[f], 1)

            def high(f, q, u):
                act.wait_ge(s_hid[f], q * (NE // 2) + u + 1)
                a.copy(hid_hi[:, 2 * u:2 * u + 2], hid[:, u % 2]).then_inc(s_hhi[f], 1)

            def swiglu(f, q, us):
                for u in us:
                    tanh(f, q, u)
                    if u:
                        high(f, q, u - 1)

            def biased(q, m):
                act.wait_ge(s_qk, q * 2 + m + 1)
                for t in range(KD):
                    ins = a.activation(qk[:, m * KD + t], att_ps[:, m, t * T:(t + 1) * T], ACT.Identity,
                                       bias=(bq4, bk_c)[m][:, t:t + 1], scale=(HD ** -0.5, 1.0)[m])
                ins.then_inc(s_qkb, 1)

            def max_turned(q):
                act.wait_ge(s_mt, q + 1)
                a.copy(nmax_t[:, :], att_side[0:3 * H, 0:P].bitcast(BF16)).then_inc(s_ms, 1)

            def exp(q, k):
                if k >= 2:
                    act.wait_ge(s_pv, q * NG + k - 1)
                for m, (c0, c1, src) in enumerate((
                        (0, HG * T, att_ps[:, 0:2, :].rearrange("p a b -> p (a b)")),
                        (HG * T, SLOT, att_ps[:, 2, :]))):
                    act.wait_ge(s_lt, q * N2 + 2 * k + m + 1)
                    a.activation(pexp[:, k % 2, c0:c1], src, ACT.Exp).then_inc(s_exp, 1)

            def copy_heads(q, half):
                act.wait_ge(s_pv, q * NG + 2 * half + 2)
                a.copy(uT[:, half], att_side[:, :]).then_inc(s_uc, 1)

            def copy_oT(q):
                act.wait_ge(s_ot, q + 1)
                a.copy(oT[:, :, :], att_ps[:, 2, :].rearrange("p (k t) -> p k t", k=KD)).then_inc(s_oT, 1)

            act.wait_ge(s_nu, 32)
            a.activation(col[:, 0:1], nu_c[:, :], ACT.Exp)
            a.activation(col[:, 1:2], th_c[:, :], ACT.Exp).then_inc(s_theta, 1)
            act.wait_ge(s_mag, 1)
            a.activation(col[:, 3:4], col[:, 2:3], ACT.Exp).then_inc(s_theta, 1)
            act.wait_ge(s_phase, 1)
            a.activation(sin_t[:, :], turn[:, 0], ACT.Sin, scale=TWO_PI)
            a.activation(cos_t[:, :], turn[:, 1], ACT.Sin, scale=TWO_PI).then_inc(s_sin, 1)
            copy_hT(0, 0)
            for m in range(3):
                act.wait_ge(s_wf[m], 16)
                if m:
                    act.wait_ge(s_abs, m)
                a.activation(absw[:, :], w_f[m][:, :], ACT.Abs, accum_out=wsum[:, m:m + 1]).then_inc(s_abs, 1)
            copy_hT(1, 0)
            act.wait_ge(s_w, 16 * len(att_weights))
            a.activation(bq4[:, :], bq_c[:, :], ACT.Copy, scale=HD ** -0.5).then_inc(s_bq, 1)
            act.wait_ge(s_bq, 1)
            act.wait_ge(s_tab, 1)
            a.activation(col[:, 13:14], k_tanh[:, 0:1], ACT.Tanh)
            swiglu(0, 0, range(2))

            def first_trip():
                copy_hT(0, 1)
                swiglu(0, 0, (2, 3))
                high(0, 0, 3)
                copy_hT(2, 0)
                biased(0, 0)
                biased(0, 1)
                copy_hT(1, 1)
                tanh(0, 1, 0)
                tanh(0, 1, 1)
                high(0, 1, 0)

            def second_trip():
                copy_hT(0, 2)
                swiglu(0, 1, (2, 3))
                high(0, 1, 3)
                copy_hT(2, 1)
                max_turned(0)
                biased(1, 0)
                copy_hT(1, 2)
                biased(1, 1)
                exp(0, 0)
                exp(0, 1)
                tanh(0, 2, 0)
                exp(0, 2)
                copy_heads(0, 0)
                exp(0, 3)
                tanh(0, 2, 1)
                copy_heads(0, 1)
                high(0, 2, 0)
                copy_oT(0)

            def trip(b, rec=True):
                if rec:
                    copy_hT(0, b + 2)
                swiglu(0, b + 1, (2, 3))
                copy_hT(3, b - 1)
                high(0, b + 1, 3)
                act.wait_ge(s_dn[0], b + 2)
                tanh(1, b - 1, 0)
                copy_hT(2, b + 1)
                tanh(1, b - 1, 1)
                max_turned(b)
                biased(b + 1, 0)
                high(1, b - 1, 0)
                biased(b + 1, 1)
                if rec:
                    copy_hT(1, b + 2)
                tanh(1, b - 1, 2)
                exp(b, 0)
                high(1, b - 1, 1)
                exp(b, 1)
                tanh(1, b - 1, 3)
                exp(b, 2)
                high(1, b - 1, 2)
                copy_heads(b, 0)
                exp(b, 3)
                high(1, b - 1, 3)
                if rec:
                    tanh(0, b + 2, 0)
                copy_heads(b, 1)
                copy_oT(b)
                if rec:
                    tanh(0, b + 2, 1)
                    act.wait_ge(s_dn[1], b)
                    high(0, b + 2, 0)

            def last_trip(b):
                copy_hT(3, b - 1)
                tanh(1, b - 1, 0)
                tanh(1, b - 1, 1)
                max_turned(b)
                high(1, b - 1, 0)
                high(1, b - 1, 1)
                tanh(1, b - 1, 2)
                tanh(1, b - 1, 3)
                exp(b, 0)
                high(1, b - 1, 2)
                exp(b, 1)
                exp(b, 2)
                copy_heads(b, 0)
                exp(b, 3)
                high(1, b - 1, 3)
                copy_heads(b, 1)
                copy_oT(b)

            first_trip()
            second_trip()
            with nc.scalar.Fori(1, B - 2) as b:
                trip(b)
            trip(B - 2, rec=False)
            last_trip(B - 1)
            copy_hT(3, B - 1)
            swiglu(1, B - 1, range(NE // 2))
            high(1, B - 1, NE // 2 - 1)

        @block.vector
        def _(dve):
            v = nc.vector
            n = [0]

            def link(ins):
                n[0] += 1
                ins.then_inc(s_prep, 1)
                dve.wait_ge(s_prep, n[0])

            def moments(m, q, src):
                for t in range(TT):
                    ins = v.bn_stats(stats[:, m, t], src[:, t])
                ins.then_inc(s_st0[m], 1)
                dve.wait_ge(s_st0[m], q + 1)
                settled(dve)
                for t in range(TT):
                    ins = v.bn_aggr(mv[:, m, t], stats[:, m, t])
                ins.then_inc(s_mv[m], 1)

            def normalise(m, q, src):
                dve.wait_ge(s_rstd[m], q + 1)
                for t in range(TT):
                    ins = v.tensor_scalar(h[m][:, t], src[:, t], mv[:, m, t, 0:1], rstd[:, m, t:t + 1],
                                          ALU.subtract, ALU.mult)
                ins.then_inc(s_h[m], 1)

            def low(m, q):
                dve.wait_ge(s_hi[m], q + 1)
                v.tensor_tensor(hT_lo[m][:, :, :], side[m][:, :].rearrange("p (k t) -> p k t", k=KD),
                                hT_hi[m][:, :, :], ALU.subtract).then_inc(s_lo[m], 1)

            def recurrence(q):
                dve.wait_ge(s_bu, q + 1)
                v.tensor_tensor(rec[:, 0], att_side[:, 0:T], rot_in[:, 0], ALU.mult)
                v.tensor_tensor(rec[:, 1], att_side[:, T:2 * T], rot_in[:, 1], ALU.mult).then_inc(s_rot, 1)
                dve.wait_ge(s_rot, q * 2 + 1)
                v.tensor_tensor(rec[:, 2], rec[:, 0], rec[:, 1], ALU.add).then_inc(s_rot, 1)
                dve.wait_ge(s_rot, q * 2 + 2)
                v.tensor_tensor_scan(rec[:, 3], decay[:, :], rec[:, 2], 0.0, ALU.mult, ALU.add).then_inc(s_rec, 1)
                dve.wait_ge(s_rec, q * 2 + 1)
                v.tensor_tensor(rec_o[:, :], rec[:, 3], rot_out[:, :], ALU.mult).then_inc(s_rec, 1)

            def residual1(q):
                dve.wait_ge(s_xd, q * TT + TT)
                dve.wait_ge(s_y, q + 1)
                v.tensor_tensor(x1[:, :, :].rearrange("p t d -> p (t d)"), att_side[:, :],
                                xd[:, :, :].rearrange("p t d -> p (t d)"), ALU.add).then_inc(s_x1, 1)
                dve.wait_ge(s_x1, q + 1)

            def hidden(f, q, ks):
                for k in ks:
                    u = k // 2
                    if k % 2 == 0:
                        dve.wait_ge(s_th[f], q * (NE // 2) + u + 1)
                        if u >= 2:
                            dve.wait_ge(s_hlo[f], q * (NE // 2) + u - 1)
                        v.scalar_tensor_tensor(up1[:, u % 2], th[:, u % 2], 1.0, ffn_ps[k % 3][:, :],
                                               ALU.add, ALU.mult).then_inc(s_up1[f], 1)
                    else:
                        dve.wait_ge(s_ug[f], q * NE + k + 1)
                        dve.wait_ge(s_up1[f], q * (NE // 2) + u + 1)
                        v.scalar_tensor_tensor(hid[:, u % 2], up1[:, u % 2], KHID, ffn_ps[k % 3][:, :],
                                               ALU.mult, ALU.mult).then_inc(s_hid[f], 1)

            def ffn_residual(f, q, src, dst):
                dve.wait_ge(s_dn[f], q + 1)
                v.scalar_tensor_tensor(dst[:, :, :].rearrange("p t d -> p (t d)"), ffn_side[:, :], k_down[:, 1:2],
                                       src[:, :, :].rearrange("p t d -> p (t d)"),
                                       ALU.mult, ALU.add).then_inc(s_res[f], 1)

            def take_v(q):
                dve.wait_ge(s_v, q + 1)
                for t in range(TT):
                    ins = v.tensor_tensor(v_s[:, t, :, 0:HD],
                                          att_ps[:, 2, t * D:(t + 1) * D].rearrange("p (h d) -> p h d", h=H),
                                          bv_b[:, :].rearrange("p (h d) -> p h d", h=H), ALU.add)
                ins.then_inc(s_vr, 1)

            def part0(q):
                dve.wait_ge(s_qkb, q * 2 + 2)
                v.tensor_copy(parts[:, 0], qk[:, :, :]).then_inc(s_p0, 1)

            def part1(q):
                dve.wait_ge(s_r1, q + 1)
                v.tensor_copy(parts[:, 1], qk_r[:, :, :]).then_inc(s_p1, 1)

            def rest1(q):
                dve.wait_ge(s_p0, q + 1)
                v.tensor_tensor(qk_r[:, :, :], qk[:, :, :], parts[:, 0], ALU.subtract).then_inc(s_r1, 1)

            def part2(q):
                dve.wait_ge(s_p1, q + 1)
                v.tensor_tensor(parts[:, 2], qk_r[:, :, :], parts[:, 1], ALU.subtract).then_inc(s_p2, 1)

            def row_max(q, g):
                hs = slice(g * HG, (g + 1) * HG)
                dve.wait_ge(s_s, q * N2 + 2 * g + 1)
                v.tensor_reduce(nmax[:, 1, hs], att_ps[:, 0:2, :].rearrange("p a (h k) -> p (a h) k", k=T), AX.X,
                                ALU.max, negate=True).then_inc(s_max, 1)
                dve.wait_ge(s_s, q * N2 + 2 * g + 2)
                v.tensor_reduce(nmax[:, 0, hs], att_ps[:, 2, :].rearrange("p (h k) -> p h k", k=P), AX.X,
                                ALU.max, negate=True).then_inc(s_max, 1)

            def max_parts(q):
                dve.wait_ge(s_max, q * N2 + N2)
                v.tensor_copy(nmax_p[:, :, 0], nmax[:, :, :]).then_inc(s_mp, 1)
                dve.wait_ge(s_mp, q * 4 + 1)
                v.tensor_tensor(nmax_r[:, :, :], nmax[:, :, :], nmax_p[:, :, 0], ALU.subtract).then_inc(s_mp, 1)
                dve.wait_ge(s_mp, q * 4 + 2)
                v.tensor_copy(nmax_p[:, :, 1], nmax_r[:, :, :]).then_inc(s_mp, 1)
                dve.wait_ge(s_mp, q * 4 + 3)
                v.tensor_tensor(nmax_p[:, :, 2], nmax_r[:, :, :], nmax_p[:, :, 1], ALU.subtract).then_inc(s_mp, 1)

            def normalise_heads(q, half):
                dve.wait_ge(s_ut, q * 2 + half + 1)
                u = att_ps[:, half, :].rearrange("p (t h e) -> p t h e", t=TT, e=2 * HD)
                hs = slice(half * H // 2, (half + 1) * H // 2)
                v.reciprocal(rsum[:, :, hs], u[:, :, :, HD]).then_inc(s_rs, 1)
                dve.wait_ge(s_rs, q * 2 + half + 1)
                for t in range(TT):
                    ins = v.tensor_tensor(o[:, t].rearrange("p (h d) -> p h d", h=H)[:, hs], u[:, t, :, 0:HD],
                                          rsum[:, t, hs].unsqueeze(2).to_broadcast([P, H // 2, HD]), ALU.mult)
                ins.then_inc(s_on, 1)

            def residual3(q, dst):
                dve.wait_ge(s_wo, q + 1)
                dve.wait_ge(s_xbo, q + 1)
                v.tensor_tensor(dst[:, :, :].rearrange("p t d -> p (t d)"), att_side[:, :],
                                x2b[:, :, :].rearrange("p t d -> p (t d)"), ALU.add).then_inc(s_x3, 1)
                dve.wait_ge(s_x3, q + 1)

            for s in range(2):
                v.memset(sgn[2 * NST * s:2 * NST * s + NST, :], 1.0)
                v.memset(sgn[2 * NST * s + NST:2 * NST * (s + 1), :], -1.0)
            dve.wait_ge(s_theta, 1)
            v.tensor_scalar(col[:, 2:3], col[:, 0:1], -1.0, -1.0, ALU.mult, ALU.add).then_inc(s_mag, 1)
            link(v.tensor_scalar(col[:, 6:7], col[:, 1:2], 0.15915494309189535, None, ALU.mult))
            link(v.tensor_scalar(col[:, 7:8], col[:, 6:7], ROUND, ROUND, ALU.add, ALU.subtract))
            link(v.tensor_tensor(col[:, 8:9], col[:, 6:7], col[:, 7:8], ALU.subtract))
            link(v.tensor_scalar(col[:, 9:10], col[:, 8:9], ROUND16, ROUND16, ALU.add, ALU.subtract))
            link(v.tensor_tensor(col[:, 10:11], col[:, 8:9], col[:, 9:10], ALU.subtract))
            dve.wait_ge(s_const, 1)
            link(v.tensor_scalar(turn[:, 0], steps[:, :], col[:, 9:10], None, ALU.mult))
            link(v.tensor_scalar(turn[:, 1], turn[:, 0], ROUND, ROUND, ALU.add, ALU.subtract))
            link(v.tensor_tensor(turn[:, 2], turn[:, 0], turn[:, 1], ALU.subtract))
            link(v.scalar_tensor_tensor(turn[:, 1], steps[:, :], col[:, 10:11], turn[:, 2], ALU.mult, ALU.add))
            link(v.tensor_scalar(turn[:, 2], turn[:, 1], ROUND, ROUND, ALU.add, ALU.subtract))
            link(v.tensor_tensor(turn[:, 0], turn[:, 1], turn[:, 2], ALU.subtract))
            dve.wait_ge(s_x, 16)
            moments(0, 0, xin)
            link(v.tensor_scalar(turn[:, 1], turn[:, 0], 0.25, None, ALU.add))
            link(v.tensor_scalar(turn[:, 2], turn[:, 1], ROUND, ROUND, ALU.add, ALU.subtract))
            v.tensor_tensor(turn[:, 1], turn[:, 1], turn[:, 2], ALU.subtract).then_inc(s_phase, 1)
            normalise(0, 0, xin)
            dve.wait_ge(s_theta, 2)
            link(v.tensor_scalar(col[:, 11:12], col[:, 3:4], col[:, 3:4], -1.0, ALU.mult, ALU.mult))
            v.tensor_scalar(col[:, 4:5], col[:, 11:12], 1.0, 0.0, ALU.add, ALU.max).then_inc(s_omg, 1)
            v.tensor_scalar(decay[:, :], steps[:, :], 0.0, col[:, 3:4], ALU.mult, ALU.add)
            dve.wait_ge(s_gam, 1)
            link(v.tensor_tensor(col[:, 12:13], col[:, 5:6], sgn[:, :], ALU.mult))
            dve.wait_ge(s_sin, 1)
            v.tensor_scalar(rot_in[:, 0], cos_t[:, :], col[:, 5:6], None, ALU.mult)
            v.tensor_scalar(rot_in[:, 1], sin_t[:, :], col[:, 12:13], None, ALU.mult)
            v.tensor_scalar(rot_out[0:2 * NST], cos_t[0:2 * NST, :], sgn[0:2 * NST, 0:1], None, ALU.mult)
            link(v.tensor_scalar(rot_out[2 * NST:], sin_t[2 * NST:, :], -1.0, None, ALU.mult))

            def threshold(m):
                dve.wait_ge(s_tot, m + 1)
                link(v.tensor_scalar(wscale[:, m:m + 1], att_ps[:, m, 0:1], 1.0 / (D * FE), Q_EPS,
                                     ALU.mult, ALU.add))
                v.tensor_scalar(whalf[:, 0, m:m + 1], wscale[:, m:m + 1], 0.5, None, ALU.mult)
                link(v.tensor_scalar(whalf[:, 1, m:m + 1], wscale[:, m:m + 1], -0.5, None, ALU.mult))
                link(v.tensor_scalar(below[:, :], w_f[m][:, :], whalf[:, 1, m:m + 1], None, ALU.is_lt))

            def quantise(m, q):
                v.scalar_tensor_tensor(q[:, :, :].rearrange("p k e -> p (k e)"), w_f[m][:, :],
                                       whalf[:, 0, m:m + 1], below[:, :], ALU.is_gt,
                                       ALU.subtract).then_inc(s_quant, 1)
                dve.wait_ge(s_quant, m + 1)

            recurrence(0)
            threshold(0)
            v.tensor_scalar(k_tanh[:, :], wscale[:, 0:1], 0.5 / UP, None, ALU.mult).then_inc(s_tab, 1)
            quantise(0, wu_q)
            residual1(0)
            moments(1, 0, x1)
            threshold(1)
            normalise(1, 0, x1)
            quantise(1, wg_q)
            low(1, 0)
            dve.wait_ge(s_x, 32)
            moments(0, 1, xin)
            threshold(2)
            hidden(0, 0, (0,))
            normalise(0, 1, xin)
            hidden(0, 0, (1,))
            quantise(2, wd_q)
            hidden(0, 0, (2, 3))

            def first_trip():
                hidden(0, 0, (4, 5, 6, 7))
                link(v.tensor_scalar(k_down[:, 0:1], wscale[:, 0:1], wscale[:, 1:2], 2.0, ALU.mult, ALU.mult))
                link(v.tensor_scalar(k_down[:, 1:2], k_down[:, 0:1], wscale[:, 2:3], None, ALU.mult))
                recurrence(1)
                ffn_residual(0, 0, x1, x2)
                dve.wait_ge(s_res[0], 1)
                moments(2, 0, x2)
                residual1(1)
                normalise(2, 0, x2)
                moments(1, 1, x1)
                dve.wait_ge(s_x, 48)
                moments(0, 2, xin)
                normalise(1, 1, x1)
                normalise(0, 2, xin)
                part0(0)
                rest1(0)
                low(1, 1)
                part1(0)
                part2(0)
                hidden(0, 1, (0,))
                take_v(0)
                hidden(0, 1, (1, 2, 3))

            def second_trip():
                hidden(0, 1, (4, 5, 6, 7))
                recurrence(2)
                row_max(0, 0)
                row_max(0, 1)
                row_max(0, 2)
                dve.wait_ge(s_xbo, 1)
                ffn_residual(0, 1, x1, x2)
                dve.wait_ge(s_res[0], 2)
                moments(2, 1, x2)
                row_max(0, 3)
                normalise(2, 1, x2)
                max_parts(0)
                residual1(2)
                moments(1, 2, x1)
                dve.wait_ge(s_x, 64)
                moments(0, 3, xin)
                normalise(1, 2, x1)
                low(1, 2)
                part0(1)
                rest1(1)
                part1(1)
                part2(1)
                hidden(0, 2, (0,))
                normalise(0, 3, xin)
                hidden(0, 2, (1, 2))
                dve.wait_ge(s_pv, NG)
                take_v(1)
                normalise_heads(0, 0)
                normalise_heads(0, 1)
                hidden(0, 2, (3,))
                residual3(0, x3)

            def trip(b, rec=True, load=True):
                row_max(b, 0)
                moments(3, b - 1, x3)
                hidden(0, b + 1, (4,))
                row_max(b, 1)
                normalise(3, b - 1, x3)
                hidden(0, b + 1, (5,))
                hidden(0, b + 1, (6, 7))
                low(3, b - 1)
                if rec:
                    recurrence(b + 2)
                row_max(b, 2)
                dve.wait_ge(s_xbo, b + 1)
                ffn_residual(0, b + 1, x1, x2)
                dve.wait_ge(s_res[0], b + 2)
                moments(2, b + 1, x2)
                if rec:
                    residual1(b + 2)
                normalise(2, b + 1, x2)
                row_max(b, 3)
                max_parts(b)
                hidden(1, b - 1, (0,))
                if rec:
                    moments(1, b + 2, x1)
                hidden(1, b - 1, (1,))
                if rec:
                    normalise(1, b + 2, x1)
                hidden(1, b - 1, (2, 3))
                part0(b + 1)
                if rec:
                    low(1, b + 2)
                hidden(1, b - 1, (4,))
                rest1(b + 1)
                hidden(1, b - 1, (5,))
                part1(b + 1)
                if load:
                    dve.wait_ge(s_x, b * 16 + 64)
                    moments(0, b + 3, xin)
                hidden(1, b - 1, (6,))
                part2(b + 1)
                hidden(1, b - 1, (7,))
                if load:
                    normalise(0, b + 3, xin)
                if rec:
                    dve.wait_ge(s_hlo[1], b * (NE // 2) - 1)
                    hidden(0, b + 2, (0,))
                dve.wait_ge(s_pv, b * NG + NG)
                take_v(b + 1)
                normalise_heads(b, 0)
                normalise_heads(b, 1)
                if rec:
                    hidden(0, b + 2, (1,))
                    dve.wait_ge(s_hlo[1], b * (NE // 2))
                    hidden(0, b + 2, (2,))
                ffn_residual(1, b - 1, x3, x4)
                dve.wait_ge(s_res[1], b)
                residual3(b, x3)
                if rec:
                    hidden(0, b + 2, (3,))

            def last_trip(b):
                moments(3, b - 1, x3)
                row_max(b, 0)
                normalise(3, b - 1, x3)
                row_max(b, 1)
                low(3, b - 1)
                row_max(b, 2)
                hidden(1, b - 1, (0,))
                row_max(b, 3)
                max_parts(b)
                hidden(1, b - 1, range(1, NE))
                normalise_heads(b, 0)
                normalise_heads(b, 1)
                residual3(b, x1)
                moments(3, b, x1)
                normalise(3, b, x1)
                ffn_residual(1, b - 1, x3, x4)

            first_trip()
            second_trip()
            with nc.vector.Fori(1, B - 3) as b:
                trip(b)
            trip(B - 3, load=False)
            trip(B - 2, load=False, rec=False)
            last_trip(B - 1)
            low(3, B - 1)
            hidden(1, B - 1, range(NE))
            dve.wait_ge(s_out, (B - 1) * 16)
            ffn_residual(1, B - 1, x1, x4)

        @block.tensor
        def _(pe):
            t_ = nc.tensor

            def transpose_norm(m, q):
                pe.wait_ge(s_h[m], q + 1)
                for t in range(TT):
                    for c in range(KD):
                        ins = t_.transpose(side[m][:, c * T + t * P:c * T + (t + 1) * P],
                                           h[m][:, t, c * P:(c + 1) * P], ident[:, :])
                ins.then_inc(s_tr[m], 1)

            def input_maps(q):
                pe.wait_ge(s_hi[0], q + 1)
                for m in range(2):
                    for c in range(KD):
                        ins = t_.matmul(att_side[:, m * T:(m + 1) * T], bu_w[:, c, m], hT[0][:, c],
                                        start=(c == 0), stop=(c == KD - 1))
                ins.then_inc(s_bu, 1)

            def output_map(q):
                pe.wait_ge(s_rec, q * 2 + 2)
                for t in range(TT):
                    ins = t_.matmul(att_side[:, t * D:(t + 1) * D], rec_o[:, t * P:(t + 1) * P], c_w[:, :],
                                    start=True, stop=True)
                ins.then_inc(s_y, 1)

            def up_gate(f, q, ks):
                m = 2 * f + 1
                if ks[0] == 0:
                    pe.wait_ge(s_hi[m], q + 1)
                    pe.wait_ge(s_lo[m], q + 1)
                for k in ks:
                    u, j = k // 2, k % 2
                    if k >= 3 and j:
                        pe.wait_ge(s_up1[f], q * (NE // 2) + u)
                    elif k >= 3:
                        pe.wait_ge(s_hid[f], q * (NE // 2) + u - 1)
                    for e in (2 * u, 2 * u + 1):
                        for c in range(KD):
                            for part, src in enumerate((hT_hi[m], hT_lo[m])):
                                ins = t_.matmul(ffn_ps[k % 3][:, e % 2], (wu_q, wg_q)[j][:, c, e * P:(e + 1) * P],
                                                src[:, c], start=(c == 0 and part == 0),
                                                stop=(c == KD - 1 and part == 1))
                    ins.then_inc(s_ug[f], 1)

            def down(f, q, t):
                for e in range(NE):
                    if t == 0 and e in (0, NE - 2):
                        pe.wait_ge(s_hlo[f], q * (NE // 2) + NE // 2 - (e == 0))
                    for part, src in enumerate((hid_hi, hid_lo)):
                        ins = t_.matmul(ffn_side[:, t * D:(t + 1) * D], src[:, e, t * P:(t + 1) * P], wd_q[:, e],
                                        start=(e == 0 and part == 0), stop=(e == NE - 1 and part == 1))
                if t == TT - 1:
                    ins.then_inc(s_dn[f], 1)

            def project(q, m):
                pe.wait_ge(s_hi[2], q + 1)
                for t in range(KD):
                    for c in range(KD):
                        ins = t_.matmul(att_ps[:, m, t * T:(t + 1) * T], (wq_s, wk_s)[m][:, c, t * P:(t + 1) * P],
                                        hT[2][:, c], start=(c == 0), stop=(c == KD - 1))
                ins.then_inc(s_qk, 1)

            def project_v(q):
                for t in range(TT):
                    for c in range(KD):
                        ins = t_.matmul(att_ps[:, 2, t * D:(t + 1) * D], hT[2][:, c, t * P:(t + 1) * P],
                                        wv_s[:, c], start=(c == 0), stop=(c == KD - 1))
                ins.then_inc(s_v, 1)

            def scores(q, g):
                if g == 0:
                    pe.wait_ge(s_st, q * ST + ST)
                    pe.wait_ge(s_vr, q + 1)
                else:
                    pe.wait_ge(s_max, q * N2 + 2 * g - 1)
                m2 = causal[:, :].unsqueeze(1).to_broadcast([P, 2, P])
                for j in range(HG // 2):
                    t_.matmul(att_ps[:, j, :].rearrange("p (h k) -> p h k", h=2)[:, :, P:T], ident_b[:, :], m2,
                              start=True, stop=False, skip_group_check=True)
                    for hh in range(2):
                        hd = g * HG + 2 * j + hh
                        ins = t_.matmul(att_ps[:, j, hh * T:(hh + 1) * T], q_st[0:CR, hd, P:T], k_st[0:CR, hd],
                                        start=False, stop=(hh == 1), skip_group_check=True)
                ins.then_inc(s_s, 1)
                if g:
                    pe.wait_ge(s_max, q * N2 + 2 * g)
                m4 = causal[:, :].unsqueeze(1).to_broadcast([P, HG, P])
                t_.matmul(att_ps[:, 2, :].rearrange("p (h k) -> p h k", h=HG), ident_b[:, :], m4,
                          start=True, stop=False, skip_group_check=True)
                for hh in range(HG):
                    hd = g * HG + hh
                    ins = t_.matmul(att_ps[:, 2, hh * P:(hh + 1) * P], q_st[0:CR, hd, 0:P], k_st[0:CR, hd, 0:P],
                                    start=False, stop=(hh == HG - 1), skip_group_check=True)
                ins.then_inc(s_s, 1)

            def turn_max(q):
                pe.wait_ge(s_mp, q * 4 + 4)
                settled(pe)
                for t in range(TT):
                    ins = t_.transpose(att_side[0:3 * H, t * P // 2:(t + 1) * P // 2].bitcast(BF16),
                                       nmax_p[:, t].rearrange("p a h -> p (a h)"), ident_b[:, :])
                ins.then_inc(s_mt, 1)

            def logits_t(q, g):
                if g == 0:
                    pe.wait_ge(s_mr, q * 48 + 48)
                    pe.wait_ge(s_max, q * N2 + N2)
                else:
                    pe.wait_ge(s_exp, q * N2 + 2 * g - 1)
                for hh in range(HG):
                    hd = g * HG + hh
                    ins = t_.matmul(att_ps[:, hh // 2, (hh % 2) * T:(hh % 2 + 1) * T], k_st[0:CR + 3, hd, 0:P],
                                    q_st[0:CR + 3, hd], start=True, stop=True)
                ins.then_inc(s_lt, 1)
                if g:
                    pe.wait_ge(s_exp, q * N2 + 2 * g)
                for hh in range(HG):
                    hd = g * HG + hh
                    ins = t_.matmul(att_ps[:, 2, hh * P:(hh + 1) * P], k_st[0:CR + 3, hd, P:T],
                                    q_st[0:CR + 3, hd, P:T], start=True, stop=True)
                ins.then_inc(s_lt, 1)

            def weigh_v(q, g):
                pe.wait_ge(s_msk, q * N2 + 2 * g + 1)
                if g == 2:
                    pe.wait_ge(s_uc, q * 2 + 1)
                c0 = (g % 2) * T
                for hh in range(HG):
                    t_.matmul(att_side[32 * hh:32 * hh + 32, c0:c0 + T], v_s[:, 0, g * HG + hh],
                              pexp[:, g % 2, hh * T:(hh + 1) * T], start=True, stop=False, skip_group_check=True)
                pe.wait_ge(s_msk, q * N2 + 2 * g + 2)
                for hh in range(HG):
                    ins = t_.matmul(att_side[32 * hh:32 * hh + 32, c0 + P:c0 + T], v_s[:, 1, g * HG + hh],
                                    pexp[:, g % 2, HG * T + hh * P:HG * T + (hh + 1) * P],
                                    start=False, stop=True, skip_group_check=True)
                ins.then_inc(s_pv, 1)

            def turn_heads(q, half):
                pe.wait_ge(s_uc, q * 2 + half + 1)
                pe.wait_ge(s_exp, q * N2 + N2)
                for t in range(TT):
                    for g in range(2):
                        c0 = t * 2 * P + g * P
                        ins = t_.transpose(att_ps[:, half, c0:c0 + P],
                                           uT[:, half, g * T + t * P:g * T + (t + 1) * P], ident[:, :])
                ins.then_inc(s_ut, 1)

            def turn_back(q):
                pe.wait_ge(s_on, q * 2 + 2)
                for t in range(TT):
                    for c in range(KD):
                        ins = t_.transpose(att_ps[:, 2, c * T + t * P:c * T + (t + 1) * P],
                                           o[:, t, c * P:(c + 1) * P], ident[:, :])
                ins.then_inc(s_ot, 1)

            def project_out(q):
                pe.wait_ge(s_oT, q + 1)
                for t in range(TT):
                    for c in range(KD):
                        ins = t_.matmul(att_side[:, t * D:(t + 1) * D], oT[:, c, t * P:(t + 1) * P], wo_s[:, c],
                                        start=(c == 0), stop=(c == KD - 1))
                ins.then_inc(s_wo, 1)

            pe.wait_ge(s_const, 1)
            transpose_norm(0, 0)
            pe.wait_ge(s_maps, 16 * len(maps))
            input_maps(0)
            pe.wait_ge(s_const, 2)

            def total(m):
                pe.wait_ge(s_abs, m + 1)
                t_.matmul(att_ps[:, m, 0:1], ones[:, :], wsum[:, m:m + 1], start=True, stop=True).then_inc(s_tot, 1)

            total(0)
            output_map(0)
            total(1)
            total(2)
            transpose_norm(1, 0)
            pe.wait_ge(s_quant, 1)
            up_gate(0, 0, (0,))
            pe.wait_ge(s_quant, 2)
            up_gate(0, 0, (1, 2, 3))
            pe.wait_ge(s_w, 16 * len(att_weights))
            pe.wait_ge(s_const, 3)

            def first_trip():
                transpose_norm(0, 1)
                up_gate(0, 0, (4, 5, 6, 7))
                input_maps(1)
                pe.wait_ge(s_quant, 3)
                down(0, 0, 0)
                down(0, 0, 1)
                output_map(1)
                transpose_norm(2, 0)
                project(0, 0)
                project(0, 1)
                pe.wait_ge(s_hi[2], 1)
                transpose_norm(1, 1)
                project_v(0)
                up_gate(0, 1, (0, 1, 2, 3))

            def second_trip():
                transpose_norm(0, 2)
                up_gate(0, 1, (4, 5, 6, 7))
                input_maps(2)
                scores(0, 0)
                down(0, 1, 0)
                scores(0, 1)
                scores(0, 2)
                down(0, 1, 1)
                scores(0, 3)
                output_map(2)
                transpose_norm(2, 1)
                pe.wait_ge(s_x1, 3)
                turn_max(0)
                pe.wait_ge(s_max, N2 - 1)
                project(1, 0)
                transpose_norm(1, 2)
                project(1, 1)
                up_gate(0, 2, (0,))
                pe.wait_ge(s_qkb, 4)
                logits_t(0, 0)
                logits_t(0, 1)
                weigh_v(0, 0)
                logits_t(0, 2)
                weigh_v(0, 1)
                up_gate(0, 2, (1,))
                logits_t(0, 3)
                weigh_v(0, 2)
                up_gate(0, 2, (2,))
                pe.wait_ge(s_exp, N2)
                project_v(1)
                weigh_v(0, 3)
                turn_heads(0, 0)
                turn_heads(0, 1)
                up_gate(0, 2, (3,))
                pe.wait_ge(s_vr, 2)
                turn_back(0)
                project_out(0)

            def trip(b, rec=True):
                pe.wait_ge(s_x3, b)
                if rec:
                    transpose_norm(0, b + 2)
                scores(b, 0)
                up_gate(0, b + 1, (4, 5))
                scores(b, 1)
                up_gate(0, b + 1, (6, 7))
                if rec:
                    input_maps(b + 2)
                transpose_norm(3, b - 1)
                scores(b, 2)
                pe.wait_ge(s_hi[3], b)
                pe.wait_ge(s_lo[3], b)
                down(0, b + 1, 0)
                down(0, b + 1, 1)
                if rec:
                    output_map(b + 2)
                scores(b, 3)
                up_gate(1, b - 1, (0, 1))
                transpose_norm(2, b + 1)
                up_gate(1, b - 1, (2,))
                pe.wait_ge(s_max, b * N2 + N2 - 1)
                project(b + 1, 0)
                if rec:
                    pe.wait_ge(s_x1, b + 3)
                turn_max(b)
                project(b + 1, 1)
                up_gate(1, b - 1, (3,))
                if rec:
                    pe.wait_ge(s_hi[2], b + 2)
                    transpose_norm(1, b + 2)
                up_gate(1, b - 1, (4,))
                pe.wait_ge(s_qkb, b * 2 + 4)
                logits_t(b, 0)
                up_gate(1, b - 1, (5,))
                logits_t(b, 1)
                weigh_v(b, 0)
                up_gate(1, b - 1, (6,))
                logits_t(b, 2)
                weigh_v(b, 1)
                up_gate(1, b - 1, (7,))
                logits_t(b, 3)
                weigh_v(b, 2)
                if rec:
                    pe.wait_ge(s_up1[1], b * (NE // 2))
                    up_gate(0, b + 2, (0,))
                weigh_v(b, 3)
                pe.wait_ge(s_exp, b * N2 + N2)
                project_v(b + 1)
                turn_heads(b, 0)
                turn_heads(b, 1)
                if rec:
                    pe.wait_ge(s_hid[1], b * (NE // 2))
                    up_gate(0, b + 2, (1,))
                down(1, b - 1, 0)
                pe.wait_ge(s_vr, b + 2)
                turn_back(b)
                if rec:
                    up_gate(0, b + 2, (2,))
                down(1, b - 1, 1)
                project_out(b)
                if rec:
                    up_gate(0, b + 2, (3,))

            def last_trip(b):
                pe.wait_ge(s_x3, b)
                scores(b, 0)
                scores(b, 1)
                transpose_norm(3, b - 1)
                scores(b, 2)
                up_gate(1, b - 1, (0, 1))
                scores(b, 3)
                up_gate(1, b - 1, (2, 3))
                turn_max(b)
                up_gate(1, b - 1, (4, 5, 6, 7))
                logits_t(b, 0)
                logits_t(b, 1)
                for g in range(NG):
                    weigh_v(b, g)
                    if g + 2 < NG:
                        logits_t(b, g + 2)
                turn_heads(b, 0)
                turn_heads(b, 1)
                turn_back(b)
                project_out(b)
                down(1, b - 1, 0)
                down(1, b - 1, 1)

            first_trip()
            second_trip()
            with nc.tensor.Fori(1, B - 2) as b:
                trip(b)
            trip(B - 2, rec=False)
            last_trip(B - 1)
            pe.wait_ge(s_res[1], B - 1)
            transpose_norm(3, B - 1)
            up_gate(1, B - 1, range(NE))
            down(1, B - 1, 0)
            down(1, B - 1, 1)


def kernel(**inputs):
    import numpy as np
    import concourse.bacc as bacc
    from concourse.bass_utils import run_bass_kernel_spmd

    a = {k.replace("L0_attn_a_", "a_").replace("L0_attn_b_", "b_").replace("L0_ffn_", "f_"): np.asarray(v)
         for k, v in inputs.items()}
    heads = lambda w: w.reshape(8, 2, 16, 256).transpose(3, 1, 2, 0).reshape(256, 256)
    bias = lambda b: b.reshape(8, 2, 16).transpose(2, 0, 1).reshape(128, 2)
    b_re, b_im, c_re, c_im = (a[k].T for k in ("a_B_re", "a_B_im", "a_C_re", "a_C_im"))
    laid = {
        "x": a["a_x"],
        "nu": np.tile(a["a_nu_log"], 4).reshape(128, 1), "theta": np.tile(a["a_theta_log"], 4).reshape(128, 1),
        "b_maps": np.stack([np.concatenate([b_re, b_im] * 2, 1), np.concatenate([b_im, b_re] * 2, 1)], 1),
        "c_maps": np.concatenate([c_re, c_im, c_im, c_re], 0),
        "d": a["a_D"],
        "wq": heads(a["b_Wq"]), "bq": bias(a["b_bq"]), "wk": heads(a["b_Wk"]), "bk": bias(a["b_bk"]),
        "wv": a["b_Wv"].T, "bv": a["b_bv"], "wo": a["b_Wo"].T, "bo": a["b_bo"],
        "w_up": a["f_W_up"].T, "w_gate": a["f_W_gate"].T, "w_down": a["f_W_down"].T,
    }
    nc = bacc.Bacc("TRN2", target_bir_lowering=False, num_devices=1)
    arrays, args = {}, []
    for name, v in laid.items():
        v = np.ascontiguousarray(v)
        arrays[f"in_{name}"] = v
        args.append(nc.dram_tensor(f"in_{name}", v.shape, mybir.dt.from_np(v.dtype), kind="ExternalInput").ap())
    args.append(nc.dram_tensor("out_0", a["a_x"].shape, mybir.dt.float32, kind="ExternalOutput").ap())
    hybrid_block_kernel(nc, *args)
    r = run_bass_kernel_spmd(nc, [arrays], core_ids=[0])
    return r.results[0]["out_0"]
```
